# Optimizing a Trainium2 kernel written in Bass

```python
import numpy as np
import jax
import jax.numpy as jnp

def _softmax(x, axis=-1):
    return jax.nn.softmax(x, axis=axis)

def _gelu(x):
    return jax.nn.gelu(x, approximate=True)

def _silu(x):
    return jax.nn.silu(x)

def _sigmoid(x):
    return jax.nn.sigmoid(x)

def _layernorm(x, axis=-1, eps=1e-05):
    m = jnp.mean(x, axis=axis, keepdims=True)
    v = jnp.var(x, axis=axis, keepdims=True)
    return (x - m) / jnp.sqrt(v + eps)

def _scatter_add(tgt, idx, src, axis=0):
    return tgt.at[idx].add(src)

def _segment_sum(src, seg, n):
    return jax.ops.segment_sum(src, seg, n)
kernel_name = 'mk_perceiver_d2_seqx_r4_f7acd6'

def setup_inputs(seed: int=0):
    np.random.seed(seed)
    _w = jnp.asarray

    def _rec_inputs():
        import jax
        import jax.numpy as jnp
        _rk = jax.random.key(seed)
        x = -0.0003929 + 0.9999 * jax.random.normal(jax.random.fold_in(_rk, 1), (2, 256, 256), jnp.float32)
        _lenS = 256 - jax.random.randint(jax.random.fold_in(_rk, 7), (2,), 0, max(1, 256 // 4) + 1, jnp.int32)
        _lenS2 = 4096 - jax.random.randint(jax.random.fold_in(_rk, 8), (2,), 0, max(1, 4096 // 4) + 1, jnp.int32)
        _ctx_1024P = jax.random.normal(jax.random.fold_in(_rk, 11), (2, 16, 256), jnp.float32)
        _ctx_1024c = jax.random.dirichlet(jax.random.fold_in(_rk, 511), 0.3 * jnp.ones((16,), jnp.float32), (2, 4096))
        _ctx_1024t = jnp.einsum('bsk,bkd->bsd', _ctx_1024c, _ctx_1024P)
        _ctx_1024t = _ctx_1024t * jax.lax.rsqrt(jnp.mean(jnp.square(_ctx_1024t)) + 1e-12) * 0.953939
        ctx_1024 = 2.81802e-05 + 1.00001 * (_ctx_1024t + 0.3 * jax.random.normal(jax.random.fold_in(_rk, 611), (2, 4096, 256), jnp.float32))
        return (x, ctx_1024)
    x, ctx_1024 = _rec_inputs()

    def _L0_xattn_setup():
        import jax, jax.numpy as jnp
        import numpy as np
        B, LQ, LKV, D = (8, 512, 512, 256)
        key = jax.random.key(seed)
        k1, k2, k3, k4, k5, k6, k7 = jax.random.split(key, 7)
        s = 1.0 / np.sqrt(D)
        return {'query': jax.random.normal(k1, (B, LQ, D), jnp.float32), 'key': jax.random.normal(k2, (B, LKV, D), jnp.float32), 'value': jax.random.normal(k3, (B, LKV, D), jnp.float32), 'Wq': jax.random.uniform(k4, (D, D), jnp.float32, -s, s), 'bq': jax.random.uniform(k5, (D,), jnp.float32, -s, s), 'Wk': jax.random.uniform(k6, (D, D), jnp.float32, -s, s), 'bk': jax.random.uniform(k7, (D,), jnp.float32, -s, s), 'scale_factor': 32, 'dropout_p': 0}
    _L0_xattn_all = _L0_xattn_setup()
    _L0_xattn_in = {k: v for k, v in _L0_xattn_all.items() if k in ('Wq', 'bq', 'Wk', 'bk')}
    del _L0_xattn_all

    def _L0_attn_setup():
        import jax, jax.numpy as jnp
        import numpy as np
        D_MODEL = 256
        N_HEADS = 64
        D_HEAD = D_MODEL // N_HEADS
        B = 2
        S = 512

        def _xavier(key, fan):
            lim = np.sqrt(6.0 / (2 * fan)).astype(np.float32)
            return jax.random.uniform(key, (fan, fan), dtype=jnp.float32, minval=-lim, maxval=lim)
        key = jax.random.key(seed)
        ks = jax.random.split(key, 9)
        blim = 1.0 / np.sqrt(D_MODEL)

        def bias(k):
            return jax.random.uniform(k, (D_MODEL,), dtype=jnp.float32, minval=-blim, maxval=blim)
        return {'x': jax.random.normal(ks[0], (B, S, D_MODEL), dtype=jnp.float32), 'Wq': _xavier(ks[1], D_MODEL), 'bq': bias(ks[2]), 'Wk': _xavier(ks[3], D_MODEL), 'bk': bias(ks[4]), 'Wv': _xavier(ks[5], D_MODEL), 'bv': bias(ks[6]), 'Wo': _xavier(ks[7], D_MODEL), 'bo': jnp.zeros((D_MODEL,), dtype=jnp.float32), 'beta': jnp.zeros((1,), dtype=jnp.float32)}
    _L0_attn_all = _L0_attn_setup()
    _L0_attn_in = {k: v for k, v in _L0_attn_all.items() if k in ('Wq', 'bq', 'Wk', 'bk', 'Wv', 'bv', 'Wo', 'bo', 'beta')}
    del _L0_attn_all

    def _L0_ffn_setup():
        import jax, jax.numpy as jnp
        import numpy as np
        B, S, DIM = (4, 1024, 256)
        BASE_COUPLING = 0.1
        NUM_CYCLES = 3

        def _gelu(x):
            return jax.nn.gelu(x, approximate=False)

        def _coupling_net(h, w1, b1, w2, b2, w3, b3, w4, b4):
            h = _gelu(h @ w1 + b1)
            h = _gelu(h @ w2 + b2)
            h = _gelu(h @ w3 + b3)
            return jax.nn.sigmoid(h @ w4 + b4)

        def _global_net(h, w1, b1, w2, b2, w3, b3):
            h = _gelu(h @ w1 + b1)
            h = _gelu(h @ w2 + b2)
            return jax.nn.sigmoid(h @ w3 + b3)

        def _twist(x):
            o_r, o_i, p_r, p_i = jnp.split(x, 4, axis=-1)
            return jnp.concatenate([p_r, -p_i, -o_r, o_i], axis=-1)
        key = jax.random.key(seed)
        ks = jax.random.split(key, 9)
        d = DIM

        def w(k, fan_in, fan_out):
            return jax.random.normal(k, (fan_in, fan_out), dtype=jnp.float32) / np.sqrt(fan_in).astype(np.float32)
        inp = {'x': jax.random.normal(ks[0], (B, S, d), dtype=jnp.float32)}
        cn_dims = [(d, d), (d, d // 2), (d // 2, d // 4), (d // 4, 1)]
        for i, (a, b) in enumerate(cn_dims):
            inp[f'cn_w{i + 1}'] = w(ks[1 + i], a, b)
            inp[f'cn_b{i + 1}'] = jnp.zeros((b,), dtype=jnp.float32)
        gc_dims = [(d, d // 2), (d // 2, d // 4), (d // 4, 1)]
        for i, (a, b) in enumerate(gc_dims):
            inp[f'gc_w{i + 1}'] = w(ks[5 + i], a, b)
            inp[f'gc_b{i + 1}'] = jnp.zeros((b,), dtype=jnp.float32)
        inp['adaptive_range'] = jnp.full((1,), 0.2, dtype=jnp.float32)
        return inp
    _L0_ffn_all = _L0_ffn_setup()
    _L0_ffn_in = {k: v for k, v in _L0_ffn_all.items() if k in ('cn_w1', 'cn_b1', 'cn_w2', 'cn_b2', 'cn_w3', 'cn_b3', 'cn_w4', 'cn_b4', 'gc_w1', 'gc_b1', 'gc_w2', 'gc_b2', 'gc_w3', 'gc_b3', 'adaptive_range')}
    del _L0_ffn_all

    def _L1_xattn_setup():
        import jax, jax.numpy as jnp
        import numpy as np
        EMBED = 256
        B, I, J = (8, 512, 512)
        SCALE = EMBED ** (-0.5)
        key = jax.random.key(seed)
        ks = jax.random.split(key, 5)
        s = EMBED ** (-0.5)
        return {'q_in': jax.random.normal(ks[0], (B, I, EMBED), dtype=jnp.float32), 'k_v': jax.random.normal(ks[1], (B, J, EMBED), dtype=jnp.float32), 'Wq': jax.random.normal(ks[2], (EMBED, EMBED), dtype=jnp.float32) * s, 'bq': jnp.zeros((EMBED,), dtype=jnp.float32), 'Wk': jax.random.normal(ks[3], (EMBED, EMBED), dtype=jnp.float32) * s, 'bk': jnp.zeros((EMBED,), dtype=jnp.float32), 'Wv': jax.random.normal(ks[4], (EMBED, EMBED), dtype=jnp.float32) * s, 'bv': jnp.zeros((EMBED,), dtype=jnp.float32)}
    _L1_xattn_all = _L1_xattn_setup()
    _L1_xattn_in = {k: v for k, v in _L1_xattn_all.items() if k in ('Wq', 'bq', 'Wk', 'bk', 'Wv', 'bv')}
    del _L1_xattn_all

    def _L1_attn_setup():
        import jax, jax.numpy as jnp
        import numpy as np
        from math import sqrt
        DIM, RANK, NHEADS = (256, 64, 16)
        B, T = (2, 512)
        key = jax.random.key(seed)
        kx, kq, kk, kv = jax.random.split(key, 4)
        QK_a = sqrt(6.0 / (RANK + DIM))
        VO_a = sqrt(6.0 / (NHEADS * DIM + DIM))
        x = jax.random.normal(kx, (B, T, DIM), dtype=jnp.float32)
        Q = jax.random.uniform(kq, (NHEADS, RANK, DIM), jnp.float32, -QK_a, QK_a)
        K = jax.random.uniform(kk, (NHEADS, RANK, DIM), jnp.float32, -QK_a, QK_a)
        VO = jax.random.uniform(kv, (NHEADS, DIM, DIM), jnp.float32, -VO_a, VO_a)
        return {'x': x, 'Q': Q, 'K': K, 'VO': VO}
    _L1_attn_all = _L1_attn_setup()
    _L1_attn_in = {k: v for k, v in _L1_attn_all.items() if k in ('Q', 'K', 'VO')}
    del _L1_attn_all

    def _L1_ffn_setup():
        import jax, jax.numpy as jnp
        import numpy as np
        D = 256
        H = 4
        HD = D // H
        E = 8
        FF = 1024
        CAP_FACTOR = 1.0

        def _ln(x, g, b, eps=1e-05):
            mu = jnp.mean(x, -1, keepdims=True)
            v = jnp.mean((x - mu) ** 2, -1, keepdims=True)
            return (x - mu) * jax.lax.rsqrt(v + eps) * g + b

        def _mha(x, w, b, ow, ob):
            L, N, _ = x.shape
            qkv = x @ w.T + b
            q, k, v = jnp.split(qkv, 3, axis=-1)
            rh = lambda t: t.reshape(L, N, H, HD).transpose(1, 2, 0, 3)
            q, k, v = (rh(q), rh(k), rh(v))
            scores = jnp.einsum('nhld,nhmd->nhlm', q, k) / np.float32(np.sqrt(HD))
            attn = jax.nn.softmax(scores, axis=-1)
            o = jnp.einsum('nhlm,nhmd->nhld', attn, v).transpose(2, 0, 1, 3).reshape(L, N, D)
            return o @ ow.T + ob

        def _moe(x, wg, w1, b1, w2, b2):
            L, N, _ = x.shape
            S = L * N
            cap = int(CAP_FACTOR * S) // E
            xf = x.reshape(S, D)
            gates = jax.nn.softmax(xf @ wg, axis=-1)
            idx = jnp.argmax(gates, axis=-1)
            mask1 = jax.nn.one_hot(idx, E, dtype=x.dtype)
            loc = jnp.sum((jnp.cumsum(mask1, 0) - 1.0) * mask1, -1).astype(jnp.int32)
            keep = loc < cap
            gate_val = jnp.take_along_axis(gates, idx[:, None], -1)[:, 0]
            slot = jnp.where(keep, idx.astype(jnp.int32) * cap + loc, E * cap)
            disp = jnp.zeros((E * cap, D), x.dtype).at[slot].set(xf, mode='drop')
            disp = disp.reshape(E, cap, D)
            h = jnp.einsum('ecd,edf->ecf', disp, w1) + b1[:, None, :]
            y = (jnp.einsum('ecf,efd->ecd', h, w2) + b2[:, None, :]).reshape(E * cap, D)
            out = jnp.where(keep[:, None], gate_val[:, None] * y[jnp.minimum(slot, E * cap - 1)], 0.0)
            return out.reshape(L, N, D)
        key = jax.random.key(seed)
        ks = jax.random.split(key, 8)
        L, N = (256, 16)
        s = 0.02
        return {'x': jax.random.normal(ks[0], (L, N, D), jnp.float32), 'in_proj_w': jax.random.normal(ks[1], (3 * D, D), jnp.float32) * s, 'in_proj_b': jnp.zeros((3 * D,), jnp.float32), 'out_proj_w': jax.random.normal(ks[2], (D, D), jnp.float32) * s, 'out_proj_b': jnp.zeros((D,), jnp.float32), 'ln1_g': jnp.ones((D,), jnp.float32), 'ln1_b': jnp.zeros((D,), jnp.float32), 'ln2_g': jnp.ones((D,), jnp.float32), 'ln2_b': jnp.zeros((D,), jnp.float32), 'wg': jax.random.normal(ks[3], (D, E), jnp.float32) * s, 'w1': jax.random.normal(ks[4], (E, D, FF), jnp.float32) * s, 'b1': jnp.zeros((E, FF), jnp.float32), 'w2': jax.random.normal(ks[5], (E, FF, D), jnp.float32) * s, 'b2': jnp.zeros((E, D), jnp.float32)}
    _L1_ffn_all = _L1_ffn_setup()
    _L1_ffn_in = {k: v for k, v in _L1_ffn_all.items() if k in ('in_proj_w', 'in_proj_b', 'out_proj_w', 'out_proj_b', 'ln1_g', 'ln1_b', 'ln2_g', 'ln2_b', 'wg', 'w1', 'b1', 'w2', 'b2')}
    del _L1_ffn_all
    return {'x': x, 'ctx_1024': ctx_1024, 'L0_xattn_Wq': _L0_xattn_in['Wq'], 'L0_xattn_bq': _L0_xattn_in['bq'], 'L0_xattn_Wk': _L0_xattn_in['Wk'], 'L0_xattn_bk': _L0_xattn_in['bk'], 'L0_attn_Wq': _L0_attn_in['Wq'], 'L0_attn_bq': _L0_attn_in['bq'], 'L0_attn_Wk': _L0_attn_in['Wk'], 'L0_attn_bk': _L0_attn_in['bk'], 'L0_attn_Wv': _L0_attn_in['Wv'], 'L0_attn_bv': _L0_attn_in['bv'], 'L0_attn_Wo': _L0_attn_in['Wo'], 'L0_attn_bo': _L0_attn_in['bo'], 'L0_attn_beta': _L0_attn_in['beta'], 'L0_ffn_cn_w1': _L0_ffn_in['cn_w1'], 'L0_ffn_cn_b1': _L0_ffn_in['cn_b1'], 'L0_ffn_cn_w2': _L0_ffn_in['cn_w2'], 'L0_ffn_cn_b2': _L0_ffn_in['cn_b2'], 'L0_ffn_cn_w3': _L0_ffn_in['cn_w3'], 'L0_ffn_cn_b3': _L0_ffn_in['cn_b3'], 'L0_ffn_cn_w4': _L0_ffn_in['cn_w4'], 'L0_ffn_cn_b4': _L0_ffn_in['cn_b4'], 'L0_ffn_gc_w1': _L0_ffn_in['gc_w1'], 'L0_ffn_gc_b1': _L0_ffn_in['gc_b1'], 'L0_ffn_gc_w2': _L0_ffn_in['gc_w2'], 'L0_ffn_gc_b2': _L0_ffn_in['gc_b2'], 'L0_ffn_gc_w3': _L0_ffn_in['gc_w3'], 'L0_ffn_gc_b3': _L0_ffn_in['gc_b3'], 'L0_ffn_adaptive_range': _L0_ffn_in['adaptive_range'], 'L1_xattn_Wq': _L1_xattn_in['Wq'], 'L1_xattn_bq': _L1_xattn_in['bq'], 'L1_xattn_Wk': _L1_xattn_in['Wk'], 'L1_xattn_bk': _L1_xattn_in['bk'], 'L1_xattn_Wv': _L1_xattn_in['Wv'], 'L1_xattn_bv': _L1_xattn_in['bv'], 'L1_attn_Q': _L1_attn_in['Q'], 'L1_attn_K': _L1_attn_in['K'], 'L1_attn_VO': _L1_attn_in['VO'], 'L1_ffn_in_proj_w': _L1_ffn_in['in_proj_w'], 'L1_ffn_in_proj_b': _L1_ffn_in['in_proj_b'], 'L1_ffn_out_proj_w': _L1_ffn_in['out_proj_w'], 'L1_ffn_out_proj_b': _L1_ffn_in['out_proj_b'], 'L1_ffn_ln1_g': _L1_ffn_in['ln1_g'], 'L1_ffn_ln1_b': _L1_ffn_in['ln1_b'], 'L1_ffn_ln2_g': _L1_ffn_in['ln2_g'], 'L1_ffn_ln2_b': _L1_ffn_in['ln2_b'], 'L1_ffn_wg': _L1_ffn_in['wg'], 'L1_ffn_w1': _L1_ffn_in['w1'], 'L1_ffn_b1': _L1_ffn_in['b1'], 'L1_ffn_w2': _L1_ffn_in['w2'], 'L1_ffn_b2': _L1_ffn_in['b2']}

def reference(x, ctx_1024, L0_xattn_Wq, L0_xattn_bq, L0_xattn_Wk, L0_xattn_bk, L0_attn_Wq, L0_attn_bq, L0_attn_Wk, L0_attn_bk, L0_attn_Wv, L0_attn_bv, L0_attn_Wo, L0_attn_bo, L0_attn_beta, L0_ffn_cn_w1, L0_ffn_cn_b1, L0_ffn_cn_w2, L0_ffn_cn_b2, L0_ffn_cn_w3, L0_ffn_cn_b3, L0_ffn_cn_w4, L0_ffn_cn_b4, L0_ffn_gc_w1, L0_ffn_gc_b1, L0_ffn_gc_w2, L0_ffn_gc_b2, L0_ffn_gc_w3, L0_ffn_gc_b3, L0_ffn_adaptive_range, L1_xattn_Wq, L1_xattn_bq, L1_xattn_Wk, L1_xattn_bk, L1_xattn_Wv, L1_xattn_bv, L1_attn_Q, L1_attn_K, L1_attn_VO, L1_ffn_in_proj_w, L1_ffn_in_proj_b, L1_ffn_out_proj_w, L1_ffn_out_proj_b, L1_ffn_ln1_g, L1_ffn_ln1_b, L1_ffn_ln2_g, L1_ffn_ln2_b, L1_ffn_wg, L1_ffn_w1, L1_ffn_b1, L1_ffn_w2, L1_ffn_b2):
    import jax
    import jax.numpy as jnp

    def _L0_xattn_ref(query, key, value, Wq, bq, Wk, bk, scale_factor, dropout_p):
        import jax, jax.numpy as jnp
        import numpy as np
        B, LQ, LKV, D = (8, 512, 512, 256)
        q = jnp.einsum('bld,ed->ble', query, Wq) + bq
        k = jnp.einsum('bld,ed->ble', key, Wk) + bk
        scores = jnp.einsum('bqd,bkd->bqk', q, k) / jnp.float32(scale_factor)
        attn = jax.nn.softmax(scores, axis=-1)
        return jnp.einsum('bqk,bkd->bqd', attn, value)

    def _L0_attn_ref(x, Wq, bq, Wk, bk, Wv, bv, Wo, bo, beta):
        import jax, jax.numpy as jnp
        import numpy as np
        D_MODEL = 256
        N_HEADS = 64
        D_HEAD = D_MODEL // N_HEADS
        B = 2
        S = 512

        def _xavier(key, fan):
            lim = np.sqrt(6.0 / (2 * fan)).astype(np.float32)
            return jax.random.uniform(key, (fan, fan), dtype=jnp.float32, minval=-lim, maxval=lim)
        b, s, dm = x.shape
        h, d = (N_HEADS, D_HEAD)

        def heads(y):
            return y.reshape(b, s, h, d).transpose(0, 2, 1, 3).reshape(b * h, s, d)
        q = heads(x @ Wq.T + bq)
        k = heads(x @ Wk.T + bk)
        v = heads(x @ Wv.T + bv)
        be = jnp.exp(beta)
        q = jax.nn.softmax(be * q, axis=-1)
        k = jax.nn.softmax(be * k, axis=-1)
        kv = jnp.cumsum(jnp.einsum('zsD,zsd->zsDd', k, v), axis=1)
        kn = jnp.cumsum(k, axis=1)
        num = jnp.einsum('zsD,zsDd->zsd', q, kv)
        den = jnp.sum(q * kn, axis=-1, keepdims=True)
        out = num / den
        out = out.reshape(b, h, s, d).transpose(0, 2, 1, 3).reshape(b, s, dm)
        return out @ Wo.T + bo

    def _L0_ffn_ref(x, cn_w1, cn_b1, cn_w2, cn_b2, cn_w3, cn_b3, cn_w4, cn_b4, gc_w1, gc_b1, gc_w2, gc_b2, gc_w3, gc_b3, adaptive_range):
        import jax, jax.numpy as jnp
        import numpy as np
        B, S, DIM = (4, 1024, 256)
        BASE_COUPLING = 0.1
        NUM_CYCLES = 3

        def _gelu(x):
            return jax.nn.gelu(x, approximate=False)

        def _coupling_net(h, w1, b1, w2, b2, w3, b3, w4, b4):
            h = _gelu(h @ w1 + b1)
            h = _gelu(h @ w2 + b2)
            h = _gelu(h @ w3 + b3)
            return jax.nn.sigmoid(h @ w4 + b4)

        def _global_net(h, w1, b1, w2, b2, w3, b3):
            h = _gelu(h @ w1 + b1)
            h = _gelu(h @ w2 + b2)
            return jax.nn.sigmoid(h @ w3 + b3)

        def _twist(x):
            o_r, o_i, p_r, p_i = jnp.split(x, 4, axis=-1)
            return jnp.concatenate([p_r, -p_i, -o_r, o_i], axis=-1)
        global_context = x.mean(axis=1, keepdims=True)
        gf = _global_net(global_context, gc_w1, gc_b1, gc_w2, gc_b2, gc_w3, gc_b3)
        out = x
        for _ in range(NUM_CYCLES):
            tf = _coupling_net(out, cn_w1, cn_b1, cn_w2, cn_b2, cn_w3, cn_b3, cn_w4, cn_b4)
            combined = 0.7 * gf + 0.3 * tf
            coupling = BASE_COUPLING + adaptive_range * (combined - 0.5) * 2.0
            out = out + coupling * _twist(out)
        return out

    def _L1_xattn_ref(q_in, k_v, Wq, bq, Wk, bk, Wv, bv):
        import jax, jax.numpy as jnp
        import numpy as np
        EMBED = 256
        B, I, J = (8, 512, 512)
        SCALE = EMBED ** (-0.5)
        q = q_in @ Wq + bq
        k = k_v @ Wk + bk
        v = k_v @ Wv + bv
        sim = jnp.einsum('bid,bjd->bij', q, k) * SCALE
        attn = jax.nn.softmax(sim, axis=-1)
        out = jnp.einsum('bij,bjd->bid', attn, v)
        return out

    def _L1_attn_ref(x, Q, K, VO):
        import jax, jax.numpy as jnp
        import numpy as np
        from math import sqrt
        DIM, RANK, NHEADS = (256, 64, 16)
        B, T = (2, 512)
        dim = x.shape[-1]
        xq = jnp.einsum('btd,hrd->bthr', x, Q)
        xk = jnp.einsum('bud,hrd->buhr', x, K)
        scores = jnp.einsum('bthr,buhr->bthu', xq, xk) / sqrt(dim)
        attn = jax.nn.softmax(scores, axis=3)
        return jnp.einsum('bthu,bud,hde->bte', attn, x, VO)

    def _L1_ffn_ref(x, in_proj_w, in_proj_b, out_proj_w, out_proj_b, ln1_g, ln1_b, ln2_g, ln2_b, wg, w1, b1, w2, b2):
        import jax, jax.numpy as jnp
        import numpy as np
        D = 256
        H = 4
        HD = D // H
        E = 8
        FF = 1024
        CAP_FACTOR = 1.0

        def _ln(x, g, b, eps=1e-05):
            mu = jnp.mean(x, -1, keepdims=True)
            v = jnp.mean((x - mu) ** 2, -1, keepdims=True)
            return (x - mu) * jax.lax.rsqrt(v + eps) * g + b

        def _mha(x, w, b, ow, ob):
            L, N, _ = x.shape
            qkv = x @ w.T + b
            q, k, v = jnp.split(qkv, 3, axis=-1)
            rh = lambda t: t.reshape(L, N, H, HD).transpose(1, 2, 0, 3)
            q, k, v = (rh(q), rh(k), rh(v))
            scores = jnp.einsum('nhld,nhmd->nhlm', q, k) / np.float32(np.sqrt(HD))
            attn = jax.nn.softmax(scores, axis=-1)
            o = jnp.einsum('nhlm,nhmd->nhld', attn, v).transpose(2, 0, 1, 3).reshape(L, N, D)
            return o @ ow.T + ob

        def _moe(x, wg, w1, b1, w2, b2):
            L, N, _ = x.shape
            S = L * N
            cap = int(CAP_FACTOR * S) // E
            xf = x.reshape(S, D)
            gates = jax.nn.softmax(xf @ wg, axis=-1)
            idx = jnp.argmax(gates, axis=-1)
            mask1 = jax.nn.one_hot(idx, E, dtype=x.dtype)
            loc = jnp.sum((jnp.cumsum(mask1, 0) - 1.0) * mask1, -1).astype(jnp.int32)
            keep = loc < cap
            gate_val = jnp.take_along_axis(gates, idx[:, None], -1)[:, 0]
            slot = jnp.where(keep, idx.astype(jnp.int32) * cap + loc, E * cap)
            disp = jnp.zeros((E * cap, D), x.dtype).at[slot].set(xf, mode='drop')
            disp = disp.reshape(E, cap, D)
            h = jnp.einsum('ecd,edf->ecf', disp, w1) + b1[:, None, :]
            y = (jnp.einsum('ecf,efd->ecd', h, w2) + b2[:, None, :]).reshape(E * cap, D)
            out = jnp.where(keep[:, None], gate_val[:, None] * y[jnp.minimum(slot, E * cap - 1)], 0.0)
            return out.reshape(L, N, D)
        y1 = _ln(x + _mha(x, in_proj_w, in_proj_b, out_proj_w, out_proj_b), ln1_g, ln1_b)
        y2 = _ln(y1 + _moe(y1, wg, w1, b1, w2, b2), ln2_g, ln2_b)
        return y2
    x = x + _L0_xattn_ref(_layernorm(x, axis=-1), ctx_1024, ctx_1024, L0_xattn_Wq, L0_xattn_bq, L0_xattn_Wk, L0_xattn_bk, 32, 0)
    x = x + _L0_attn_ref(_layernorm(x, axis=-1), L0_attn_Wq, L0_attn_bq, L0_attn_Wk, L0_attn_bk, L0_attn_Wv, L0_attn_bv, L0_attn_Wo, L0_attn_bo, L0_attn_beta)
    x = x + _L0_ffn_ref(_layernorm(x, axis=-1), L0_ffn_cn_w1, L0_ffn_cn_b1, L0_ffn_cn_w2, L0_ffn_cn_b2, L0_ffn_cn_w3, L0_ffn_cn_b3, L0_ffn_cn_w4, L0_ffn_cn_b4, L0_ffn_gc_w1, L0_ffn_gc_b1, L0_ffn_gc_w2, L0_ffn_gc_b2, L0_ffn_gc_w3, L0_ffn_gc_b3, L0_ffn_adaptive_range)
    x = x + _L1_xattn_ref(_layernorm(x, axis=-1), ctx_1024, L1_xattn_Wq, L1_xattn_bq, L1_xattn_Wk, L1_xattn_bk, L1_xattn_Wv, L1_xattn_bv)
    x = x + _L1_attn_ref(_layernorm(x, axis=-1), L1_attn_Q, L1_attn_K, L1_attn_VO)
    x = x + _L1_ffn_ref(_layernorm(x, axis=-1), L1_ffn_in_proj_w, L1_ffn_in_proj_b, L1_ffn_out_proj_w, L1_ffn_out_proj_b, L1_ffn_ln1_g, L1_ffn_ln1_b, L1_ffn_ln2_g, L1_ffn_ln2_b, L1_ffn_wg, L1_ffn_w1, L1_ffn_b1, L1_ffn_w2, L1_ffn_b2)
    return x

_drawn_inputs = setup_inputs


def setup_inputs(seed=0):
    import zlib

    import numpy as np

    out = dict(_drawn_inputs(seed))
    spreads = {'L0_attn_bo': (0.0, 0.1),
     'L0_ffn_cn_b1': (0.0, 2.0),
     'L0_ffn_cn_b2': (0.0, 2.0),
     'L0_ffn_cn_b3': (0.0, 2.0),
     'L0_ffn_gc_b1': (0.0, 2.0),
     'L0_ffn_gc_b2': (0.0, 2.0),
     'L1_xattn_bq': (0.0, 0.786),
     'L1_xattn_bk': (0.0, 2.0),
     'L1_xattn_bv': (0.0, 0.1),
     'L1_ffn_in_proj_b': (0.0, 0.8),
     'L1_ffn_out_proj_b': (0.0, 0.278),
     'L1_ffn_ln1_g': (1.0, 0.2),
     'L1_ffn_ln1_b': (0.0, 0.288),
     'L1_ffn_ln2_g': (1.0, 0.2),
     'L1_ffn_ln2_b': (0.0, 0.1),
     'L1_ffn_b1': (0.0, 0.8),
     'L1_ffn_b2': (0.0, 2.0)}
    factors = {'L0_xattn_bq': 8.0,
     'L0_xattn_bk': 64.0,
     'L0_attn_bq': 8.0,
     'L0_attn_bk': 8.0,
     'L0_ffn_cn_w1': 8.0,
     'L0_ffn_cn_w2': 8.0,
     'L0_ffn_cn_w3': 8.0,
     'L0_ffn_cn_w4': 8.0,
     'L0_ffn_gc_w1': 4.199,
     'L0_ffn_gc_w2': 8.0,
     'L0_ffn_gc_w3': 3.211,
     'L1_ffn_in_proj_w': 2.678,
     'L1_ffn_wg': 5.754,
     'L1_ffn_w1': 6.353,
     'L1_ffn_w2': 6.194}
    for name, (base, spread) in spreads.items():
        noise = np.random.default_rng([zlib.crc32(name.encode()), seed]).standard_normal(out[name].shape)
        drawn = base * np.exp(spread * noise) if base else spread * noise
        out[name] = jnp.asarray(drawn.astype(out[name].dtype))
    for name, factor in factors.items():
        out[name] = (out[name] * factor).astype(out[name].dtype)
    return out
```

```python
from contextlib import ExitStack
from itertools import chain
import math

import numpy as np
import concourse.bass as bass
from concourse import mybir

ALU = mybir.AluOpType
ACT = mybir.ActivationFunctionType
AX = mybir.AxisListType
F32 = mybir.dt.float32
F16 = mybir.dt.float16
U32 = mybir.dt.uint32

P = 128
B, SEQ, D = 2, 256, 256
N = B * SEQ
NT = N // P
DC = D // P
KV = 4096
CH = 512
NCH = KV // CH
KT = CH // P
NG = B * NCH
NU = NT
NJ = NU * NCH
SRING = 11
AHEAD = 3
TURN = 2
PRING = 3
EPS = 1e-5
SHIFT = 10 * math.log(2.0)
VO_SCALE = 64.0
SCALES = (1.0 / 32, 1.0 / 16)
H2, D2 = 64, 4
H5 = 16
H6, HD6 = 4, 64
E6, FF, CAP = 8, 1024, 64
FC = FF // P
CYCLES = 3

COLS = ["x_bq0", "x_bq1", "x_bk0", "x_bk1", "y_bq0", "y_bq1", "y_bk0", "y_bk1", "cn_b1_0", "cn_b1_1", "cn_b2",
        "cn_b3", "cn_b4", "gc_b1", "gc_b2", "gc_b3", "beta", "ar", "sgn0", "sgn1", "neghalf"]
COL = {n: i for i, n in enumerate(COLS)}

NORMS = [("x", 0), ("x", 1), ("a", 0), ("f", 0), ("y", 0), ("a", 1), ("f", 1), ("y", 1), ("l", 0), ("l", 1), ("m", 0),
         ("m", 1)]
NORM = {n: i for i, n in enumerate(NORMS)}
POOL_CUTS = NCH
LA_WAIT = 4


def steps_of(order):
    return [(kind, u, c) for kind, u, c0, c1 in order for c in range(c0, c1)]


ORDER = steps_of([step for u in range(0, NU, 2) for step in (
    ("S", u, 0, 8), ("S", u + 1, 0, 3), ("A", u, 0, 4), ("S", u + 1, 3, 8), ("A", u, 4, 8), ("A", u + 1, 0, 8))])
PREP_AT = [0, 1, 2, 3, 4, 5, 6, 8, 11, 14, 16, 23, 25, 27, 29]
SIDE_AT = (
    [7, 8, 11, 13, 15, 64, 66, 70, 72, 72, 74, 74, 78, 78, 80, 80, 80, 85, 86, 92, 92, 93, 93, 95, 102, 104,
     104, 104, 105, 105, 108, 108, 108, 108, 108, 110, 110, 110, 111, 111, 113, 113, 117, 118, 122, 125],
    [0, 1, 4, 6, 6, 9, 10, 10, 12, 16, 17, 18, 23, 23, 27, 30, 33, 33, 35, 39, 42, 42, 42, 43, 43, 46, 47, 50,
     51, 51, 52, 52, 53, 53, 53, 54, 54, 57, 60, 62, 62, 80, 84, 92, 94, 97, 99, 110, 111, 112, 113, 117],
)


def acc_bank(u):
    return 6 if u % 2 == 0 else 1


def side_banks(what, b=0):
    return (4, 5, 7) if what == "x" else (2, 3, 7) if (what, b) != ("l", 1) else (4, 5, 7)


def side_steps(L, half, steps):
    for _ in range(SIDE_AT[L].count(half)):
        next(steps, None)


def ahead(order, i, n):
    j = i + n
    return order[j][1:] if 0 <= j < len(order) and order[j][0] == "A" else None


def finishes(order, i, n):
    j = i - n
    return order[j][1] if 0 <= j < len(order) and order[j][0] == "A" and order[j][2] == NCH - 1 else None


def build(nc, x, ctx, consts, cols, w_x, w_a, w_ao, b_a, w_f1, w_f2, w_f3, w_f4, w_g1, w_g2, w_g3, w_y, w_yv, b_yv,
          w_l, w_vo, w_in, w_out, rows6, w_gate, w_e1, b_e1, w_e2, b_e2, consts6, out):
    with ExitStack() as stack:
        def sb(name, shape, dt=F32):
            return stack.enter_context(nc.sbuf_tensor(name, shape, dt))

        sems = {}

        def s(name):
            if name not in sems:
                sems[name] = stack.enter_context(nc.semaphore(name))
            return sems[name]

        ps = stack.enter_context(nc.psum_tensor("ps", [P, 8, 512], F32))

        def bank(i, **dims):
            return ps[:, i, :] if not dims else ps[:, i, :].rearrange("p (a b) -> p a b", **dims)

        ctx_nat = sb("ctx_nat", [P, B * KV // P * D])
        ctx_tr = sb("ctx_tr", [P, DC * B * KV])
        arena = sb("arena", [P, 8192])
        work = sb("work", [P, 4096])
        wts = sb("wts", [P, 4224])
        X = sb("X", [P, NT, D])
        pth = sb("pth", [P, 2, CH], F16)
        ptl = sb("ptl", [P, 2, CH], F16)
        qtl = sb("qtl", [P, 2, DC, N], F16)
        const = sb("const", [P, 3, P])
        ident, tri, tris = const[:, 0, :], const[:, 1, :], const[:, 2, :]
        ones = sb("ones", [P, P])
        col = sb("col", [P, len(COLS)])
        w41 = sb("w41", [64, 2])
        bst = sb("bst", [P, 2, 6])
        mv = sb("mv", [P, 2, 2])
        rstd = sb("rstd", [P, 2])
        mx = sb("mx", [P, NU, NCH])
        ls = sb("ls", [P, NU, NCH])
        small = sb("small", [P, 64])
        rq, rqs, mrow, negb, ebias, lsum, rl = (small[:, 4 * i:4 * i + 4] for i in range(7))
        tg, cA, cB, cA7, g1s, g2s, becol, b4h, b3h = (small[:, 28 + i:29 + i] for i in range(9))
        gsum = small[:, 37:39]

        CN = ctx_nat[:, :].bitcast(F16).rearrange("p (t h d) -> p t h d", h=2, d=D)
        CT = ctx_tr[:, :].bitcast(F16).rearrange("p (c h k) -> p c h k", c=DC, h=2)
        S = arena[:, 0:SRING * CH].rearrange("p (n k) -> p n k", n=SRING)
        pt3 = arena[:, SRING * CH:(SRING + 1) * CH].bitcast(F16).rearrange("p (h k) -> p h k", h=2)
        PH, PL = [pth[:, 0], pth[:, 1], pt3[:, 0]], [ptl[:, 0], ptl[:, 1], pt3[:, 1]]
        stage = work[:, 0:2048].rearrange("p (r t d) -> p r t d", r=2, d=D)
        xn = work[:, 2048:2560].rearrange("p (t d) -> p t d", d=D)
        xnT = work[:, 2560:3072].rearrange("p (c n) -> p c n", c=DC)
        qT = work[:, 3072:3584].rearrange("p (c n) -> p c n", c=DC)
        ident16 = work[:, 3584:3648].bitcast(F16)
        on = work[:, 3584:3840]
        onT = work[:, 3840:4096].rearrange("p (c n) -> p c n", c=DC)
        wa = arena[:, 6144:7680].rearrange("p (c n) -> p c n", c=DC)
        wao = arena[:, 7680:8192].rearrange("p (c n) -> p c n", c=DC)
        F2 = work[:, 0:2048].rearrange("p (t f) -> p t f", t=2)
        qk2 = [work[:, 3072:3584], work[:, 2048:2560]]
        v2 = work[:, 3584:4096].rearrange("p (t d) -> p t d", t=2)
        t2 = work[:, 2560:3072]
        s2 = sb("s2", [P, P])
        h1, h2, h3 = work[:, 0:512].rearrange("p (c n) -> p c n", c=2), work[:, 512:768], work[0:64, 768:1024]
        th, cpl, tw = work[:, 1024:1280], work[:, 1280:1536], work[:, 1536:2048].rearrange("p (c n) -> p c n", c=2)

        def cut(a, shape, **dims):
            n = int(np.prod(shape))
            ap = wts[0:P, a:a + n]
            return ap if len(shape) == 1 else ap.rearrange("p (c n) -> p c n", c=shape[0])

        wx = wts[:, 0:1024].rearrange("p (w c n) -> p w c n", w=2, c=DC)
        ba = wts[:, 1024:2048]
        wyv = cut(2048, (DC, D))
        byv = wts[:, 2560:2816]
        wf1 = cut(2816, (DC, D))
        wf2 = cut(3328, (DC, P))
        wf3 = wts[:, 3584:3648]
        wf4 = wts[0:64, 3648:3776]
        wg1 = cut(3776, (DC, P))
        wg2 = wts[:, 4032:4096]
        wg3 = wts[0:64, 4096:4224]

        wl_stage = ctx_nat[:, 0:4096].rearrange("p (j n) -> p j n", j=H5 // 2)
        wl = ctx_nat[:, 4096:8192].bitcast(F16).rearrange("p (j h n) -> p j h n", j=H5 // 2, h=2)
        QL5 = ctx_tr[:, 0:4096].bitcast(F16).rearrange("p (h j n) -> p h j n", h=2, j=H5 // 2)
        KL5 = ctx_tr[:, 4096:12288].bitcast(F16).rearrange("p (h j e n) -> p h j e n", h=2, j=H5 // 2, e=2)
        xl5 = [a.bitcast(F16).rearrange("p (h t d) -> p h t d", h=2, t=2) for a in (wts[:, 0:512], ctx_tr[:, 12800:13312])]
        xT5 = work[:, 2560:3584].bitcast(F16).rearrange("p (h c n) -> p h c n", h=2, c=DC)
        P5 = ctx_tr[:, 14336:15360].rearrange("p (r t u) -> p r t u", r=2, t=2)
        oT5 = ctx_tr[:, 15360:16384].bitcast(F16).rearrange("p (r h c n) -> p r h c n", r=2, h=2, c=DC)
        vo = arena[:, :].bitcast(F16).rearrange("p (n h c d) -> p n h c d", n=H5, h=2, c=DC)
        vo_stage = work[:, 0:2048].rearrange("p (h c n) -> p h c n", h=4, c=DC)
        nb5, l5 = small[:, 40:44].rearrange("p (r t) -> p r t", r=2), small[:, 44:48].rearrange("p (r t) -> p r t", r=2)

        tail, rest = ctx_tr[:, 12288:16384], arena[:, 4096:8192]
        w1 = ctx_nat[:, :].rearrange("p (e c f) -> p e c f", e=E6, c=DC)
        w2 = [ctx_tr[:, 2048 * e:2048 * e + 2048] if e < 6 else arena[:, 2048 * (e - 6):2048 * (e - 5)] for e in range(E6)]
        w2 = [w.rearrange("p (f n) -> p f n", f=FC) for w in w2]
        w6i = work[:, 0:1536].rearrange("p (c n) -> p c n", c=DC)
        w6o = work[:, 1536:2048].rearrange("p (c n) -> p c n", c=DC)
        r6 = wts[:, 0:2048]
        b6i, b6o, ln1g, ln1b, ln2g, ln2b = (r6[:, a:z] for a, z in ((0, 768), (768, 1024), (1024, 1280), (1280, 1536),
                                                                    (1536, 1792), (1792, 2048)))
        b2r = wts[:, 2816:3840].rearrange("p (g n) -> p g n", g=E6 // 2)
        wgt = wts[:, 3840:3856].rearrange("p (c n) -> p c n", c=DC)
        b1c = wts[:, 3856:3920].rearrange("p (e f) -> p e f", e=E6)
        x0 = tail[:, 0:1024].rearrange("p (t d) -> p t d", t=NT)
        x0T = tail[:, 1024:2048].rearrange("p (c n) -> p c n", c=DC)
        o6 = tail[:, 2048:3072].rearrange("p (t d) -> p t d", t=NT)
        oT6 = tail[:, 3072:4096].rearrange("p (c n) -> p c n", c=DC)
        qkv = ctx_nat[:, 12288:15360].rearrange("p (t n) -> p t n", t=NT)
        prods = [rest[:, 3072:4096], rest[:, 2048:3072]]
        Sm = rest[:, 0:1024].bitcast(F16).rearrange("p (t n) -> p t n", t=NT)
        ST = rest[:, 1024:2048].bitcast(F16).rearrange("p (g n) -> p g n", g=E6 // 2)
        y1 = tail[:, 3072:4096].bitcast(F16).rearrange("p (h t d) -> p h t d", h=2, t=NT)
        disT = tail[:, 2048:3072].rearrange("p (c n) -> p c n", c=DC)
        yy = tail[:, 3072:4096].bitcast(F16).rearrange("p (g h n) -> p g h n", g=E6 // 2, h=2)
        hh = [tail[:, 1024:2048], work[:, 3072:4096]]
        hT = [rest[:, 2048 + 1024 * i:3072 + 1024 * i].rearrange("p (f n) -> p f n", f=FC) for i in range(2)]
        ys = rest[:, 0:256]
        iota, rev, e64 = work[:, 3072:3584], work[:, 3584:3592], work[:, 3592:3600]
        by_batch = lambda a, j: a.rearrange("p c (b t n) -> p c b t n", b=B, t=2)[:, :, :, j, :]
        id16 = s2[:, 0:64].bitcast(F16)
        m_ = work[:, 2560:3072]
        bst4 = m_[:, 0:24].rearrange("p (t k) -> p t k", t=NT)
        mv4 = m_[:, 24:32].rearrange("p (t k) -> p t k", t=NT)
        rstd4, m8, gate, slot, mw, head, over = (m_[:, 32 + 4 * i:36 + 4 * i] for i in range(7))
        sc = m_[:, 64:96].rearrange("p (j l m h) -> p j l m h", j=2, l=2, m=2)
        smx = m_[:, 96:112].rearrange("p (j l h) -> p j l h", j=2, l=2)
        lg, e8, t8, u8 = (m_[:, 128 + 32 * i:160 + 32 * i].rearrange("p (t e) -> p t e", t=NT) for i in range(4))
        oh = m_[:, 256:272].bitcast(F16).rearrange("p (t e) -> p t e", t=NT)
        ones16, tris16 = (m_[:, 288 + 64 * i:352 + 64 * i].bitcast(F16) for i in range(2))

        x_tiles = x.rearrange("(t p) d -> p t d", p=P)
        ctx_tiles = ctx.rearrange("(g t p) d -> g p t d", p=P, t=KT)
        out_tiles = out.rearrange("(t p) d -> p t d", p=P)

        def queries_times_keys(engine, j):
            q = qkv[:, j:NT:2, 0:256].unsqueeze(2).broadcast_to([P, 2, 2, D])
            k = qkv[:, j:NT:2, 256:512].unsqueeze(1).broadcast_to([P, 2, 2, D])
            return engine.tensor_tensor(prods[j].rearrange("p (l m d) -> p l m d", l=2, m=2), q, k, ALU.mult)

        block = stack.enter_context(nc.Block())

        @block.sync
        def _(sp):
            sp.dma_start(X[:, 0:2, :], x_tiles[:, 0:2]).then_inc(s("x_in0"), 16)
            sp.dma_start(const[:, :, :], consts).then_inc(s("const_in"), 16)
            sp.dma_start(col[:, :], cols).then_inc(s("const_in"), 16)
            sp.dma_start(wx, w_x).then_inc(s("wx_in"), 16)
            for g in range(NG):
                if g >= 2:
                    sp.wait_ge(s("ctx_hi"), g - 1)
                    sp.wait_ge(s("ctx_lo"), g - 1)
                sp.dma_start(stage[:, g % 2], ctx_tiles[g]).then_inc(s("ctx_in%d" % (g % 2)), 16)
                if g == 1:
                    sp.dma_start(X[:, 2:4, :], x_tiles[:, 2:4]).then_inc(s("x_in1"), 16)
                if g == 3:
                    sp.dma_start(wa, w_a).then_inc(s("wa_in"), 16)
                    sp.dma_start(wao, w_ao).then_inc(s("wa_in"), 16)
                    sp.dma_start(ba, b_a.partition_broadcast(P)).then_inc(s("wa_in"), 16)
                if g == 6:
                    for dst, src in ((wf1, w_f1), (wf2, w_f2), (wf3, w_f3), (wg1, w_g1),
                                     (wg2, w_g2), (w41[:, 0:1], w_f4), (w41[:, 1:2], w_g3)):
                        sp.dma_start(dst, src).then_inc(s("wf_in"), 16)
            sp.wait_ge(s("px_qt"), 2)
            sp.dma_start(wx, w_y).then_inc(s("wx_in"), 16)
            sp.dma_start(wyv, w_yv).then_inc(s("wyv_in"), 16)
            sp.dma_start(byv, b_yv.partition_broadcast(P)).then_inc(s("wyv_in"), 16)
            sp.wait_ge(s("av"), NJ + 2 * NCH)
            for j in range(4):
                sp.dma_start(wl_stage[:, 2 * j:2 * j + 2], w_l[:, 2 * j:2 * j + 2].rearrange("p j c n -> p j (c n)"))\
                    .then_inc(s("wl_in%d" % j), 16)
            load_w1 = lambda e: sp.dma_start(w1[:, e], w_e1[e].rearrange("(c p) f -> p c f", p=P)).then_inc(s("w1_in%d" % e), 16)
            load_w2 = lambda e: sp.dma_start(w2[e], w_e2[e].rearrange("(f p) d -> p f d", p=P)).then_inc(s("w2_in%d" % e), 16)
            def load_vo(q):
                if q >= 2:
                    sp.wait_ge(s("vo_hi"), 2 * q - 2)
                    sp.wait_ge(s("vo_lo"), 2 * q - 2)
                sp.dma_start(vo_stage[:, 2 * (q % 2):2 * (q % 2) + 2], w_vo[2 * q:2 * q + 2].rearrange("h (c p) n -> p h c n", p=P))\
                    .then_inc(s("vo_in%d" % (q % 2)), 16)

            sp.wait_ge(s("qt_lo"), 2 * B)
            load_vo(0)
            load_vo(1)
            sp.wait_ge(s("av"), 2 * NJ)
            for e in range(4, 6):
                load_w1(e)
            for q in range(2, H5 // 2):
                load_vo(q)
            sp.wait_ge(s("vo_hi"), H5)
            sp.wait_ge(s("vo_lo"), H5)
            for dst, src in ((w6i, w_in), (w6o, w_out), (wgt, w_gate), (b1c, b_e1)):
                sp.dma_start(dst, src).then_inc(s("w6_in"), 16)
            for e in range(E6):
                sp.dma_start(b2r[64 * (e % 2):64 * (e % 2) + 64, e // 2, :], b_e2[e].partition_broadcast(64)).then_inc(s("w6_in"), 16)
            sp.wait_ge(s("l_proj"), H5)
            sp.dma_start(work[:, 3072:3600], consts6).then_inc(s("w6_in"), 16)
            for e in range(4):
                load_w1(e)
            sp.wait_ge(s("l_pv"), H5)
            sp.dma_start(r6, rows6.partition_broadcast(P)).then_inc(s("w6_in"), 16)
            sp.wait_ge(s("l_vo"), H5 + H5 // 2)
            load_w2(6)
            load_w2(7)
            sp.wait_ge(s("l_pv"), 2 * H5)
            for e in range(6):
                load_w2(e)
            sp.wait_ge(s("m_o"), 2)
            load_w1(6)
            load_w1(7)
            for b in range(B):
                sp.wait_ge(s("x_final"), b + 1)
                sp.dma_start(out_tiles[:, 2 * b:2 * b + 2], X[:, 2 * b:2 * b + 2, :]).then_inc(s("stored"), 16)
            sp.wait_ge(s("stored"), 16 * B)

        @block.tensor
        def _(pe):
            def turn_norm(what, b):
                k = NORM[what, b]
                pe.wait_ge(s("xn"), k + 1)
                if k == 0:
                    pe.wait_ge(s("const_in"), 32)
                for c in range(DC):
                    for t in range(2):
                        mm = pe.transpose(ps[:, side_banks(what, b)[0], (c * 2 + t) * P:(c * 2 + t + 1) * P],
                                          xn[:, t, c * P:(c + 1) * P], ident)
                mm.then_inc(s("xn_turned"), 1)

            def project(what, b):
                k = (what == "y") * B + b
                b0, b1, b2 = side_banks(what)
                yield
                yield
                turn_norm(what, b)
                yield
                pe.wait_ge(s("xnT"), NORM[what, b] + 1)
                pe.wait_ge(s("wx_in"), 16 if what == "x" else 32)
                for e in range(DC):
                    for c in range(DC):
                        mm = pe.matmul(ps[:, b1, e * SEQ:(e + 1) * SEQ], wx[:, 0, c, e * P:(e + 1) * P], xnT[:, c, :],
                                       start=(c == 0), stop=(c == DC - 1))
                mm.then_inc(s("px_q"), 1)
                yield
                pe.wait_ge(s("qT"), k + 1)
                bk = COL[what + "_bk0"]
                for t in range(2):
                    for e in range(DC):
                        pe.matmul(ps[:, b0, t:t + 1], qT[:, e, t * P:(t + 1) * P], col[:, bk + e:bk + e + 1],
                                  start=(e == 0), stop=(e == DC - 1))
                for c in range(DC):
                    for e in range(DC):
                        mm = pe.matmul(ps[:, b2, c * SEQ:(c + 1) * SEQ], wx[:, 1, e, c * P:(c + 1) * P], qT[:, e, :],
                                       start=(e == 0), stop=(e == DC - 1))
                mm.then_inc(s("px_qt"), 1)
                yield

            def linear_attention(b):
                yield
                yield
                turn_norm("a", b)
                yield
                pe.wait_ge(s("xnT"), NORM["a", b] + 1)
                pe.wait_ge(s("wa_in"), 48)
                lhs = lambda t, c: xnT[:, c, t * P:(t + 1) * P]
                for t in range(2):
                    for c in range(DC):
                        pe.matmul(ps[:, 3, t * D:(t + 1) * D], lhs(t, c), wa[:, c, 512:768], start=(c == 0), stop=(c == DC - 1))
                for t in range(2):
                    for c in range(DC):
                        mm = pe.matmul(ps[:, 2 if t == 0 else 7, :], lhs(t, c), wa[:, c, 0:512],
                                       start=(c == 0), stop=(c == DC - 1))
                    mm.then_inc(s("a_qkv"), 1)
                    yield
                for _ in range(LA_WAIT):
                    yield
                for t in range(2):
                    pe.wait_ge(s("a_F"), 2 * b + t + 1)
                    if t:
                        pe.wait_ge(s("a_o"), 2 * b + 1)
                    for i, (o, f) in enumerate(((ps[:, 2, :], lambda r: F2[:, r, 0:512]), (ps[:, 3, :], lambda r: F2[:, r, 512:1024]),
                                                (ps[:, 7, 0:D], lambda r: qk2[r][:, D:2 * D]))):
                        if t:
                            pe.matmul(o, ones[:, :], f(0), start=True, stop=False)
                        mm = pe.matmul(o, tri, f(t), start=(t == 0), stop=True)
                    mm.then_inc(s("a_cum"), 1)
                    yield
                    yield
                    yield
                pe.wait_ge(s("a_o"), 2 * b + 2)
                for c in range(DC):
                    for t in range(2):
                        mm = pe.transpose(ps[:, 2, (c * 2 + t) * P:(c * 2 + t + 1) * P], v2[:, t, c * P:(c + 1) * P], ident)
                mm.then_inc(s("a_oT_ps"), 1)
                yield
                pe.wait_ge(s("a_oT"), b + 1)
                for t in range(2):
                    for c in range(DC):
                        mm = pe.matmul(ps[:, 3, t * D:(t + 1) * D], t2[:, (c * 2 + t) * P:(c * 2 + t + 1) * P], wao[:, c, :],
                                       start=(c == 0), stop=(c == DC - 1))
                mm.then_inc(s("a_out"), 1)
                yield

            def feed_forward(b):
                yield
                yield
                turn_norm("f", b)
                yield
                pe.wait_ge(s("xnT"), NORM["f", b] + 1)
                pe.wait_ge(s("wf_in"), 112)
                for i in range(CYCLES):
                    n = b * CYCLES + i
                    if i:
                        pe.wait_ge(s("f_x"), n)
                    for m in range(2):
                        for c in range(DC):
                            mm = pe.matmul(ps[:, 2, m * SEQ:(m + 1) * SEQ], wf1[:, c, m * P:(m + 1) * P], xnT[:, c, :],
                                           start=(c == 0), stop=(c == DC - 1))
                    mm.then_inc(s("f_1"), 1)
                    if i == 0:
                        pe.wait_ge(s("f_sum"), b + 1)
                        for c in range(DC):
                            mm = pe.matmul(ps[:, 7, 0:1], wg1[:, c, :], gsum[:, c:c + 1], start=(c == 0), stop=(c == DC - 1))
                        mm.then_inc(s("f_g"), 1)
                    yield
                    pe.wait_ge(s("f_h1"), n + 1)
                    for c in range(2):
                        mm = pe.matmul(ps[:, 3, 0:SEQ], wf2[:, c, :], h1[:, c, :], start=(c == 0), stop=(c == 1))
                    mm.then_inc(s("f_2"), 1)
                    if i == 0:
                        pe.wait_ge(s("f_gs"), 3 * b + 1)
                        pe.matmul(ps[0:64, 7, 1:2], wg2, g1s, start=True, stop=True).then_inc(s("f_g"), 1)
                    yield
                    pe.wait_ge(s("f_h2"), n + 1)
                    pe.matmul(ps[0:64, 3, SEQ:2 * SEQ], wf3, h2, start=True, stop=True).then_inc(s("f_3"), 1)
                    if i == 0:
                        pe.wait_ge(s("f_gs"), 3 * b + 2)
                        pe.wait_ge(s("wrep"), 2)
                        pe.matmul(ps[:, 7, 2:3], wg3, g2s[0:64, :], start=True, stop=True).then_inc(s("f_g"), 1)
                    yield
                    pe.wait_ge(s("f_h3"), n + 1)
                    if i == 0:
                        pe.wait_ge(s("f_gs"), 3 * b + 3)
                    pe.matmul(ps[:, 7, SEQ:2 * SEQ], wf4, h3, start=True, stop=True).then_inc(s("f_4"), 1)
                    yield
                    yield
                pe.wait_ge(s("f_x"), (b + 1) * CYCLES)
                for t in range(2):
                    for c in range(DC):
                        mm = pe.transpose(ps[:, 2, (t * 2 + c) * P:(t * 2 + c + 1) * P], xnT[:, c, t * P:(t + 1) * P], ident)
                mm.then_inc(s("f_back"), 1)
                yield

            def side(b):
                yield from linear_attention(b)
                yield from feed_forward(b)
                yield from project("y", b)

            def prep(g):
                pe.wait_ge(s("ctx_hi"), g + 1)
                pe.wait_ge(s("ctx_lo"), g + 1)
                if g >= 1:
                    pe.wait_ge(s("ctT_hi"), g)
                    pe.wait_ge(s("ctT_lo"), g)
                for h in range(2):
                    to = ps[:, 2 + h, :].bitcast(F16).rearrange("p (c k) -> p c k", c=DC)
                    for t in range(KT):
                        for c in range(DC):
                            mm = pe.transpose(to[:, c, t * P:(t + 1) * P], CN[:, g * KT + t, h, c * P:(c + 1) * P],
                                              ident16[:, :])
                mm.then_inc(s("ctT_ps"), 1)

            def scores(L, u, c, midway):
                n, b = L * NJ + u * NCH + c, u // 2
                if c == 0 and u % 2 == 0:
                    pe.wait_ge(s("qt_lo"), B * L + b + 1)
                    pe.wait_ge(s("qt_hi"), B * L + b + 1)
                if L == 0:
                    pe.wait_ge(s("ctT_hi"), b * NCH + c + 1)
                    pe.wait_ge(s("ctT_lo"), b * NCH + c + 1)
                if n >= 2:
                    pe.wait_ge(s("score_copied"), n - 1)
                if c == 1 and u % 2 == 0 and L * NU + u:
                    pe.wait_ge(*((s("y_on"), u) if L and u else (s("acc_free"), L * NU + u)))
                k0 = b * KV + c * CH
                for i, (qh, kh) in enumerate(((0, 0), (0, 1), (1, 0))):
                    for d in range(DC):
                        if (i, d) == (1, 1):
                            midway()
                        mm = pe.matmul(ps[:, n % 2, :], qtl[:, qh, d, u * P:(u + 1) * P], CT[:, d, kh, k0:k0 + CH],
                                       start=(i == 0 and d == 0), stop=(i == 2 and d == DC - 1))
                mm.then_inc(s("score"), 1)

            def turn(L, u, c):
                j = L * NJ + u * NCH + c
                pe.wait_ge(s("exp"), j + 1)
                if j >= 2:
                    pe.wait_ge(s("pt_hi"), j - 1)
                    pe.wait_ge(s("pt_lo"), j - 1)
                else:
                    pe.wait_ge(s("qt_lo"), B)
                for i in range(KT):
                    mm = pe.transpose(ps[:, 4 + j % 2, i * P:(i + 1) * P], S[:, (j) % SRING, i * P:(i + 1) * P], ident)
                mm.then_inc(s("pt"), 1)

            def values(L, u, c, midway):
                j = L * NJ + u * NCH + c
                pe.wait_ge(s("pt_lo"), j + 1)
                acc = acc_bank(u)
                if c == 0 and u % 2:
                    pe.wait_ge(s("score_copied"), L * NJ + (u + 1) * NCH)
                elif c == 0 and L * NU + u:
                    pe.wait_ge(s("acc_free"), L * NU + u)
                for i in range(KT):
                    t = (u // 2) * (KV // P) + c * KT + i
                    if i == KT // 2:
                        midway()
                    pe.matmul(ps[:, acc, :], PH[j % PRING][:, i * P:(i + 1) * P], CN[:, t].rearrange("p h d -> p (h d)"),
                              start=(c == 0 and i == 0), stop=False, skip_group_check=True)
                    mm = pe.matmul(ps[:, acc, 0:D], PL[j % PRING][:, i * P:(i + 1) * P], CN[:, t, 0, :],
                                   start=False, stop=(c == NCH - 1 and i == KT - 1), skip_group_check=True)
                mm.then_inc(s("av"), 1)

            def finish_turn(u):
                pe.wait_ge(s("y_on"), u + 1)
                if u:
                    pe.wait_ge(s("acc_free"), NU + u)
                for c in range(DC):
                    mm = pe.transpose(ps[:, 6, c * P:(c + 1) * P], on[:, c * P:(c + 1) * P], ident)
                mm.then_inc(s("y_onT_ps"), 1)

            def finish_v(u):
                pe.wait_ge(s("y_onT"), u + 1)
                pe.wait_ge(s("wyv_in"), 32)
                for c in range(DC):
                    mm = pe.matmul(ps[:, 6, D:2 * D], onT[:, c, :], wyv[:, c, :], start=(c == 0), stop=(c == DC - 1))
                mm.then_inc(s("y_v"), 1)

            def attend(L, side_of):
                order = ORDER
                for i, (kind, u, c) in enumerate(order):
                    if L == 0 and i in PREP_AT:
                        prep(PREP_AT.index(i) + 1)
                    if ahead(order, i, TURN):
                        turn(L, *ahead(order, i, TURN))
                    if kind == "S":
                        scores(L, u, c, lambda: side_steps(L, 2 * i, side_of))
                    else:
                        values(L, u, c, lambda: side_steps(L, 2 * i, side_of))
                    if L == 1 and finishes(order, i, 1) is not None:
                        finish_turn(finishes(order, i, 1))
                    if L == 1 and finishes(order, i, 2) is not None:
                        finish_v(finishes(order, i, 2))
                    if L == 1 and i + 1 == len(order):
                        finish_turn(u)
                        finish_v(u)
                    side_steps(L, 2 * i + 1, side_of)
                for _ in side_of:
                    pass

            def enter_low_rank():
                yield
                yield
                turn_norm("l", 0)
                for _ in range(1 + H5 // 2):
                    yield

            def low_rank_attention():
                for b in range(B):
                    pe.wait_ge(s("xnT"), NORM["l", b] + 1)
                    for j in range(H5 // 2):
                        n = b * (H5 // 2) + j
                        pe.wait_ge(s("wl_lo"), j + 1)
                        if n >= 4:
                            pe.wait_ge(s("l_lo"), n - 3)
                        for i in range(2):
                            for c in range(DC):
                                for k, (wh, xh) in enumerate(((0, 0), (0, 1), (1, 0))):
                                    mm = pe.matmul(ps[:, n % 4, i * SEQ:(i + 1) * SEQ], wl[:, j, wh, (2 * c + i) * P:(2 * c + i + 1) * P],
                                                   xT5[:, xh, c, b * SEQ:(b + 1) * SEQ], start=(c == 0 and k == 0),
                                                   stop=(c == DC - 1 and k == 2))
                        mm.then_inc(s("l_proj"), 1)
                        if n == 2:
                            turn_norm("l", 1)
                def scores5(i):
                    h, b = i % H5, i // H5
                    if i >= 2:
                        pe.wait_ge(s("l_exp"), 2 * (i - 1))
                    for t in range(2):
                        for n, (qh, kh) in enumerate(((0, 0), (0, 1), (1, 0))):
                            mm = pe.matmul(ps[:, i % 2, t * SEQ:(t + 1) * SEQ],
                                           QL5[:, qh, h // 2, b * SEQ + t * P:b * SEQ + (t + 1) * P],
                                           KL5[:, kh, h // 2, h % 2, b * SEQ:(b + 1) * SEQ], start=(n == 0), stop=(n == 2))
                    mm.then_inc(s("l_score"), 1)

                def turn5(i):
                    pe.wait_ge(s("l_norm"), i + 1)
                    if i >= 2:
                        pe.wait_ge(s("l_pt_lo"), i - 1)
                    for u in range(2):
                        for t in range(2):
                            mm = pe.transpose(ps[:, 2 + i % 2, (2 * u + t) * P:(2 * u + t + 1) * P],
                                              P5[:, i % 2, t, u * P:(u + 1) * P], ident)
                    mm.then_inc(s("l_pt"), 1)

                def mix5(i):
                    b = i // H5
                    pe.wait_ge(s("l_pt_lo"), i + 1)
                    if i >= 2:
                        pe.wait_ge(s("l_ot_lo"), i - 1)
                    for d in range(DC):
                        n = 0
                        for u in range(2):
                            pu = slice(u * SEQ, (u + 1) * SEQ)
                            for xh, pt in ((0, pth), (1, pth), (0, ptl)):
                                mm = pe.matmul(ps[:, 4 + i % 2, d * SEQ:(d + 1) * SEQ], xl5[b][:, xh, u, d * P:(d + 1) * P],
                                               pt[:, i % 2, pu], start=(n == 0), stop=(n == 5))
                                n += 1
                    mm.then_inc(s("l_pv"), 1)

                def out5(i):
                    h, b = i % H5, i // H5
                    pe.wait_ge(s("l_ot_lo"), i + 1)
                    pe.wait_ge(s("vo_lo"), h + 1)
                    for t in range(2):
                        for c in range(DC):
                            for n, (oh, vh) in enumerate(((0, 0), (0, 1), (1, 0))):
                                mm = pe.matmul(ps[:, 6 + b, t * D:(t + 1) * D], oT5[:, i % 2, oh, c, t * P:(t + 1) * P],
                                               vo[:, h, vh, c, :], start=(h == 0 and t == 0 and c == 0 and n == 0),
                                               stop=(h == H5 - 1 and c == DC - 1 and n == 2), skip_group_check=True)
                    mm.then_inc(s("l_vo"), 1)

                early = enter_last()
                pe.wait_ge(s("l_lo"), H5)
                pe.wait_ge(s("l_zero"), 4)
                pe.wait_ge(s("l_x_lo"), B)
                for i in range(2 * H5 + 4):
                    if i < 2 * H5:
                        scores5(i)
                    if 0 <= i - 2 < 2 * H5:
                        turn5(i - 2)
                    if 0 <= i - 3 < 2 * H5:
                        mix5(i - 3)
                    if 0 <= i - 4 < 2 * H5:
                        out5(i - 4)
                    if i >= H5 + 4:
                        next(early, None)

            def turn_pair(src, j, n0, name):
                for c in range(DC):
                    for b in range(B):
                        mm = pe.transpose(ps[:, n0 + j, (c * 2 + b) * P:(c * 2 + b + 1) * P],
                                          src[:, 2 * b + j, c * P:(c + 1) * P], ident)
                mm.then_inc(s(name), 1)

            def turn_latents(b, to):
                pe.wait_ge(s("xn"), NORM["m", b] + 1)
                for c in range(DC):
                    for t in range(2):
                        mm = pe.transpose(ps[:, to, (c * 2 + t) * P:(c * 2 + t + 1) * P], x0[:, 2 * b + t, c * P:(c + 1) * P], ident)
                mm.then_inc(s("xn_turned"), 1)

            def enter_last():
                for _ in range(3):
                    yield
                turn_latents(0, 6)
                yield
                pe.wait_ge(s("m_xT"), 1)
                pe.wait_ge(s("w6_in"), 16 * 14)
                for n in range(4):
                    t, cols = n // 2, ((0, 512), (512, 768))[n % 2]
                    if n:
                        pe.wait_ge(s("m_qkv0"), n)
                    for c in range(DC):
                        mm = pe.matmul(ps[:, 6, 0:cols[1] - cols[0]], x0T[:, c, t * P:(t + 1) * P], w6i[:, c, cols[0]:cols[1]],
                                       start=(c == 0), stop=(c == DC - 1))
                    mm.then_inc(s("m_qkv0_ps"), 1)
                    yield

            def last_attention():
                turn_latents(1, 3)
                pe.wait_ge(s("m_xT"), 2)
                for j in range(2):
                    t, n0 = 2 + j, 4 * j
                    for c in range(DC):
                        pe.matmul(ps[:, n0, :], x0T[:, c, t * P:(t + 1) * P], w6i[:, c, 0:512], start=(c == 0), stop=(c == DC - 1))
                    for c in range(DC):
                        mm = pe.matmul(ps[:, n0 + 1, 0:D], x0T[:, c, t * P:(t + 1) * P], w6i[:, c, 512:768],
                                       start=(c == 0), stop=(c == DC - 1))
                    mm.then_inc(s("m_qkv_ps"), 1)
                for j in range(2):
                    pe.wait_ge(s("m_o"), j + 1)
                    turn_pair(o6, j, 6, "m_oT_ps")
                    pe.wait_ge(s("m_oT"), j + 1)
                    for b in range(B):
                        t = 2 * b + j
                        for c in range(DC):
                            mm = pe.matmul(ps[:, 2 + j, b * D:(b + 1) * D], oT6[:, c, t * P:(t + 1) * P],
                                           w6o[:, c, :], start=(c == 0), stop=(c == DC - 1))
                    mm.then_inc(s("m_out"), 1)

            def experts():
                for j in range(2):
                    pe.wait_ge(s("m_y1"), j + 1)
                    turn_pair(x0, j, 4, "m_yT_ps")
                for j in range(2):
                    pe.wait_ge(s("m_yT"), j + 1)
                    for t in (j, 2 + j):
                        for c in range(DC):
                            mm = pe.matmul(ps[:, 6, t * E6:(t + 1) * E6], x0T[:, c, t * P:(t + 1) * P], wgt[:, c, :],
                                           start=(c == 0), stop=(c == DC - 1))
                mm.then_inc(s("m_logit"), 1)
                pe.wait_ge(s("m_oh"), 1)
                pe.wait_ge(s("id16"), 1)
                pe.matmul(ps[:, 7, 0:NT * E6], tris16, oh.rearrange("p t e -> p (t e)"), start=True, stop=False, skip_group_check=True)
                for k in range(1, NT):
                    mm = pe.matmul(ps[:, 7, k * E6:NT * E6], ones16, oh[:, 0:NT - k, :].rearrange("p t e -> p (t e)"),
                                   start=False, stop=(k == NT - 1), skip_group_check=True)
                mm.then_inc(s("m_cum"), 1)
                pe.wait_ge(s("m_y1_lo"), 2)
                pe.wait_ge(s("id16"), 1)
                for t in range(NT):
                    pe.wait_ge(s("m_S"), t + 1)
                    for c in range(DC):
                        for h in range(2):
                            mm = pe.matmul(ps[:, c, :], y1[:, h, t, c * P:(c + 1) * P], Sm[:, t, :], start=(t == 0 and h == 0),
                                           stop=(t == NT - 1 and h == 1))
                        if t == NT - 1:
                            mm.then_inc(s("m_dis_ps"), 1)
                for g in range(E6 // 2):
                    to = ps[:, 2 + g, 0:SEQ].bitcast(F16)
                    for t in range(NT):
                        mm = pe.transpose(to[:, t * P:(t + 1) * P], Sm[:, t, g * P:(g + 1) * P], id16)
                    mm.then_inc(s("m_ST_ps"), 1)

                def hidden(g):
                    if g == 0:
                        pe.wait_ge(s("m_dis"), 2)
                    else:
                        pe.wait_ge(s("m_h"), 2 * g)
                    for e in (2 * g, 2 * g + 1):
                        pe.wait_ge(s("w1_in%d" % e), 16)
                        o = 64 * (e % 2)
                        for f in range(2):
                            for c in range(DC):
                                mm = pe.matmul(ps[o:o + 64, f, :], disT[:, c, e * CAP:(e + 1) * CAP],
                                               w1[:, e, c, f * 512:(f + 1) * 512], start=(c == 0), stop=(c == DC - 1))
                    mm.then_inc(s("m_h_ps"), 1)

                def turn_hidden(g):
                    pe.wait_ge(s("m_h"), 2 * g + 2)
                    if g == 0:
                        pe.wait_ge(s("m_ST"), 4)
                    else:
                        pe.wait_ge(s("m_hT"), 2 * g)
                    for f in range(FC):
                        mm = pe.transpose(ps[:, 2 + f // 4, (f % 4) * P:(f % 4 + 1) * P], hh[g % 2][:, f * P:(f + 1) * P], ident)
                    mm.then_inc(s("m_hT_ps"), 1)

                def down(g):
                    if g:
                        pe.wait_ge(s("m_y"), g)
                    for half, e in ((0, 2 * g), (0, 2 * g + 1), (1, 2 * g), (1, 2 * g + 1)):
                        pe.wait_ge(s("m_hT"), 2 * g + 1 + half)
                        pe.wait_ge(s("w2_in%d" % e), 16)
                        o = 64 * (e % 2)
                        for f in range(half * FC // 2, (half + 1) * FC // 2):
                            mm = pe.matmul(ps[o:o + 64, 4, 0:D], hT[g % 2][:, f, o:o + 64], w2[e][:, f, :],
                                           start=(f == 0), stop=(f == FC - 1), skip_group_check=True)
                    mm.then_inc(s("m_y_ps"), 1)

                def combine(g):
                    pe.wait_ge(s("m_y"), g + 1)
                    for b in range(B):
                        for t in (2 * b, 2 * b + 1):
                            for h in range(2):
                                mm = pe.matmul(ps[:, 6 + b, (t % 2) * D:(t % 2 + 1) * D], ST[:, g, t * P:(t + 1) * P], yy[:, g, h],
                                               start=(g == 0 and t % 2 == 0 and h == 0), stop=(g == E6 // 2 - 1 and h == 1),
                                               skip_group_check=True)
                        if g == E6 // 2 - 1:
                            mm.then_inc(s("m_comb"), 1)

                G = E6 // 2
                hidden(0)
                for g in range(G):
                    turn_hidden(g)
                    if g + 1 < G:
                        hidden(g + 1)
                    down(g)
                    if g:
                        combine(g - 1)
                combine(G - 1)

            first = project("x", 0)
            for _ in range(4):
                next(first)
            prep(0)
            for _ in first:
                pass
            attend(0, chain(project("x", 1), side(0)))
            attend(1, chain(side(1), enter_low_rank()))
            low_rank_attention()
            last_attention()
            experts()

        @block.scalar
        def _(act):
            def project(what, b):
                k = (what == "y") * B + b
                yield
                yield
                yield
                yield
                act.wait_ge(s("px_qt"), k + 1)
                if k >= 2:
                    act.wait_ge(s("score"), (b + 1) * 2 * NCH)
                act.activation(qtl[:, 0, :, b * SEQ:(b + 1) * SEQ], bank(7, a=DC), ACT.Copy).then_inc(s("qt_hi"), 1)
                yield

            def linear_attention(b):
                yield
                yield
                yield
                yield
                for t in range(2):
                    yield
                    act.wait_ge(s("a_sub"), 2 * b + t + 1)
                    act.activation(qk2[t], qk2[t], ACT.Exp, scale=becol).then_inc(s("a_exp"), 1)
                for _ in range(LA_WAIT - 1):
                    yield
                for t in range(2):
                    yield
                    yield
                    yield
                act.wait_ge(s("a_oT_ps"), b + 1)
                act.activation(t2, ps[:, 2, :], ACT.Copy).then_inc(s("a_oT"), 1)
                yield
                yield

            def feed_forward(b):
                yield
                yield
                yield
                for i in range(CYCLES):
                    n = b * CYCLES + i
                    act.wait_ge(s("f_1"), n + 1)
                    if n >= 1:
                        act.wait_ge(s("f_2"), n)
                    if i == 0:
                        act.wait_ge(s("a_cum"), 2 * b + 2)
                    for m in range(2):
                        o = act.activation(h1[:, m, :], ps[:, 2, m * SEQ:(m + 1) * SEQ], ACT.Gelu, bias=C("cn_b1_%d" % m))
                    o.then_inc(s("f_h1"), 1)
                    if i == 0:
                        act.wait_ge(s("f_g"), 3 * b + 1)
                        act.activation(g1s, ps[:, 7, 0:1], ACT.Gelu, bias=C("gc_b1"), scale=1.0 / SEQ).then_inc(s("f_gs"), 1)
                    yield
                    act.wait_ge(s("f_2"), n + 1)
                    act.activation(h2, ps[:, 3, 0:SEQ], ACT.Gelu, bias=C("cn_b2")).then_inc(s("f_h2"), 1)
                    if i == 0:
                        act.wait_ge(s("f_g"), 3 * b + 2)
                        act.activation(g2s[0:64, :], ps[0:64, 7, 1:2], ACT.Gelu, bias=C("gc_b2", 64)).then_inc(s("f_gs"), 1)
                    yield
                    act.wait_ge(s("f_3"), n + 1)
                    act.activation(h3, ps[0:64, 3, SEQ:2 * SEQ], ACT.Gelu, bias=C("cn_b3", 64)).then_inc(s("f_h3"), 1)
                    if i == 0:
                        act.wait_ge(s("f_g"), 3 * b + 3)
                        if b:
                            act.wait_ge(s("f_cA"), b)
                        act.activation(tg, ps[:, 7, 2:3], ACT.Tanh, bias=b3h, scale=0.5).then_inc(s("f_gs"), 1)
                    yield
                    act.wait_ge(s("f_4"), n + 1)
                    if n >= 1:
                        act.wait_ge(s("f_x"), n)
                    act.activation(th, ps[:, 7, SEQ:2 * SEQ], ACT.Tanh, bias=b4h, scale=0.5).then_inc(s("f_th"), 1)
                    yield
                    yield
                yield

            def side(b):
                yield from linear_attention(b)
                yield from feed_forward(b)
                yield from project("y", b)

            def cut_hi(g):
                act.wait_ge(s("ctx_in%d" % (g % 2)), 16 * (g // 2 + 1))
                act.activation(CN[:, g * KT:(g + 1) * KT, 0, :], stage[:, g % 2], ACT.Copy).then_inc(s("ctx_hi"), 1)

            def prep_out(g):
                act.wait_ge(s("ctT_ps"), g + 1)
                act.activation(CT[:, :, 0, g * CH:(g + 1) * CH],
                               ps[:, 2, :].bitcast(F16).rearrange("p (c k) -> p c k", c=DC), ACT.Copy).then_inc(s("ctT_hi"), 1)

            def exp(L, u, c):
                j = L * NJ + u * NCH + c
                if c == 0:
                    act.wait_ge(s("ebias"), L * NU + u + 1)
                    act.wait_ge(s("score_copied"), L * NJ + (u + 1) * NCH)
                act.activation(S[:, j % SRING, :], S[:, j % SRING, :], ACT.Exp, bias=ebias[:, u:u + 1],
                               scale=SCALES[L], accum_out=ls[:, u, c:c + 1]).then_inc(s("exp"), 1)

            def pt_hi(L, u, c):
                j = L * NJ + u * NCH + c
                act.wait_ge(s("pt"), j + 1)
                if j >= PRING:
                    act.wait_ge(s("av"), j - PRING + 1)
                act.activation(PH[j % PRING], ps[:, 4 + j % 2, :], ACT.Copy).then_inc(s("pt_hi"), 1)

            def score_copy(L, u, c):
                n = L * NJ + u * NCH + c
                act.wait_ge(s("score"), n + 1)
                if n >= SRING:
                    act.wait_ge(s("pt"), n - SRING + 1)
                act.activation(S[:, n % SRING, :], ps[:, n % 2, :], ACT.Copy).then_inc(s("score_copied"), 1)

            def attend(L, side_of):
                order = ORDER
                for i, (kind, u, c) in enumerate(order):
                    if ahead(order, i, AHEAD):
                        exp(L, *ahead(order, i, AHEAD))
                    if L == 0 and i in PREP_AT:
                        g = PREP_AT.index(i) + 1
                        if g + 1 < NG:
                            cut_hi(g + 1)
                        prep_out(g)
                    if ahead(order, i, TURN):
                        pt_hi(L, *ahead(order, i, TURN))
                    side_steps(L, 2 * i, side_of)
                    if kind == "S":
                        score_copy(L, u, c)
                    side_steps(L, 2 * i + 1, side_of)
                for _ in side_of:
                    pass

            def x_hi(b):
                act.wait_ge(s("xn"), NORM["l", b] + 1)
                act.activation(xl5[b][:, 0], xn, ACT.Copy).then_inc(s("l_x_hi"), 1)

            def xT_hi(b):
                act.wait_ge(s("xn_turned"), NORM["l", b] + 1)
                act.activation(xT5[:, 0, :, b * SEQ:(b + 1) * SEQ], bank(side_banks("l", b)[0], a=DC), ACT.Copy).then_inc(s("l_xT_hi"), 1)

            def enter_low_rank():
                yield
                yield
                x_hi(0)
                xT_hi(0)
                yield
                for j in range(H5 // 2):
                    act.wait_ge(s("wl_in%d" % (j // 2)), 16)
                    act.activation(wl[:, j, 0], wl_stage[:, j], ACT.Copy).then_inc(s("wl_hi"), 1)
                    yield

            def low_rank_attention():
                def vo_hi(h):
                    act.wait_ge(s("vo_in%d" % (h // 2 % 2)), 16 * (h // 4 + 1))
                    act.activation(vo_stage[:, h % 4], vo_stage[:, h % 4], ACT.Copy, scale=VO_SCALE).then_inc(s("vo_scaled"), 1)
                    act.wait_ge(s("vo_scaled"), h + 1)
                    act.activation(vo[:, h, 0], vo_stage[:, h % 4], ACT.Copy).then_inc(s("vo_hi"), 1)

                act.wait_ge(s("av"), 2 * NJ)
                for b in range(B):
                    cols = slice(b * SEQ, (b + 1) * SEQ)
                    for j in range(H5 // 2):
                        n = b * (H5 // 2) + j
                        act.wait_ge(s("l_proj"), n + 1)
                        act.activation(QL5[:, 0, j, cols], ps[:, n % 4, 0:SEQ], ACT.Copy)
                        for e in range(2):
                            r = slice(64 * e, 64 * e + 64)
                            o = act.activation(KL5[r, 0, j, e, cols], ps[r, n % 4, SEQ:2 * SEQ], ACT.Copy)
                        o.then_inc(s("l_hi"), 1)
                        if n == 2:
                            x_hi(1)
                            xT_hi(1)
                        if n in (7, 9, 11):
                            vo_hi((n - 7) // 2)

                def exp5(i):
                    act.wait_ge(s("l_max"), i + 1)
                    if i >= 2:
                        act.wait_ge(s("l_pt"), i - 1)
                    for t in range(2):
                        act.activation(P5[:, i % 2, t, :], ps[:, i % 2, t * SEQ:(t + 1) * SEQ], ACT.Exp, bias=nb5[:, i % 2, t:t + 1],
                                       scale=1.0 / 16, accum_out=l5[:, i % 2, t:t + 1]).then_inc(s("l_exp"), 1)

                def hi5(i):
                    act.wait_ge(s("l_pt"), i + 1)
                    if i >= 2:
                        act.wait_ge(s("l_pv"), i - 1)
                    act.activation(pth[:, i % 2, :], ps[:, 2 + i % 2, :], ACT.Copy).then_inc(s("l_pt_hi"), 1)

                def oT(i):
                    act.wait_ge(s("l_pv"), i + 1)
                    if i >= 2:
                        act.wait_ge(s("l_vo"), i - 1)
                    act.activation(oT5[:, i % 2, 0], bank(4 + i % 2, a=DC), ACT.Copy).then_inc(s("l_ot_hi"), 1)

                for i in range(2 * H5 + 4):
                    if i < 2 * H5:
                        exp5(i)
                    if 0 <= i - 2 < 2 * H5:
                        hi5(i - 2)
                    if 0 <= i - 3 < 2 * H5:
                        oT(i - 3)
                    if i + 3 < H5:
                        vo_hi(i + 3)

            def last_part():
                def y_hi(g):
                    act.wait_ge(s("m_ys"), g + 1)
                    act.activation(yy[:, g, 0], ys, ACT.Copy).then_inc(s("m_y_hi"), 1)

                for j in range(2):
                    act.wait_ge(s("m_sub"), j + 1)
                    act.activation(sc[:, j], sc[:, j], ACT.Exp, scale=HD6 ** -0.5).then_inc(s("m_exp"), 1)
                    act.wait_ge(s("m_oT_ps"), j + 1)
                    act.activation(by_batch(oT6, j), ps[:, 6 + j, :].rearrange("p (c b n) -> p c b n", c=DC, b=B), ACT.Copy)\
                        .then_inc(s("m_oT"), 1)
                for j in range(2):
                    act.wait_ge(s("m_yT_ps"), j + 1)
                    act.activation(by_batch(x0T, j), ps[:, 4 + j, :].rearrange("p (c b n) -> p c b n", c=DC, b=B), ACT.Copy)\
                        .then_inc(s("m_yT"), 1)
                for j in range(2):
                    act.activation(y1[:, 0, j:NT:2, :], x0[:, j:NT:2, :], ACT.Copy).then_inc(s("m_y1_hi"), 1)
                act.wait_ge(s("m_sub8"), 1)
                act.activation(e8, e8, ACT.Exp).then_inc(s("m_exp8"), 1)
                act.wait_ge(s("m_dis_ps"), 1)
                act.activation(disT[:, 0, :], ps[:, 0, :], ACT.Copy).then_inc(s("m_dis"), 1)
                for g in (0, 2):
                    act.wait_ge(s("m_ST_ps"), g + 1)
                    act.activation(ST[:, g, :], ps[:, 2 + g, 0:SEQ].bitcast(F16), ACT.Copy).then_inc(s("m_ST"), 1)
                for g in range(E6 // 2):
                    act.wait_ge(s("m_h_ps"), g + 1)
                    if g >= 2:
                        act.wait_ge(s("m_hT_ps"), g - 1)
                    act.activation(hh[g % 2][:, 0:512], ps[:, 0, :], ACT.Copy).then_inc(s("m_h"), 1)
                    if g:
                        y_hi(g - 1)
                y_hi(E6 // 2 - 1)

            C = lambda name, n=P: col[0:n, COL[name]:COL[name] + 1]
            act.wait_ge(s("const_in"), 32)
            act.activation(becol, C("beta"), ACT.Exp).then_inc(s("becol"), 1)
            act.wait_ge(s("becol"), 1)
            act.wait_ge(s("halves"), 1)
            cut_hi(0)
            cut_hi(1)
            prep_out(0)
            for _ in project("x", 0):
                pass
            attend(0, chain(project("x", 1), side(0)))
            attend(1, chain(side(1), enter_low_rank()))
            low_rank_attention()
            last_part()

        @block.gpsimd
        def _(pool):
            def layernorm(what, b):
                pool.wait_ge(s("var"), NORM[what, b] + 1)
                nh = col[:, COL["neghalf"]:COL["neghalf"] + 1].broadcast_to([P, 2])
                pool.tensor_tensor(rstd[:, :], mv[:, :, 1], nh, ALU.pow).then_inc(s("rstd"), 1)

            def linear_attention(b):
                layernorm("a", b)
                for t in range(2):
                    n = 2 * b + t
                    pool.wait_ge(s("a_soft"), n + 1)
                    f4 = F2[:, t, :].rearrange("p (h a d) -> p h a d", a=D2, d=D2)
                    k4 = qk2[t][:, D:2 * D].rearrange("p (h a) -> p h a", a=D2).unsqueeze(3).broadcast_to([P, H2, D2, D2])
                    v4 = v2[:, t, :].rearrange("p (h d) -> p h d", d=D2).unsqueeze(2).broadcast_to([P, H2, D2, D2])
                    pool.tensor_tensor(f4, k4, v4, ALU.mult).then_inc(s("a_F"), 1)

            pool.wait_ge(s("const_in"), 32)
            for b in range(B):
                layernorm("x", b)
            for g in range(POOL_CUTS, NG):
                pool.wait_ge(s("ctx_in%d" % (g % 2)), 16 * (g // 2 + 1))
                pool.wait_ge(s("ctx_hi"), g + 1)
                if g == POOL_CUTS:
                    pool.wait_ge(s("ctx_lo"), g)
                pool.tensor_tensor(CN[:, g * KT:(g + 1) * KT, 1, :], stage[:, g % 2], CN[:, g * KT:(g + 1) * KT, 0, :],
                                   ALU.subtract).then_inc(s("ctx_lo"), 1)
            for b in range(B):
                linear_attention(b)
                layernorm("f", b)
                layernorm("y", b)
            layernorm("l", 0)
            for j in range(H5 // 2):
                pool.wait_ge(s("wl_hi"), j + 1)
                pool.tensor_tensor(wl[:, j, 1], wl_stage[:, j], wl[:, j, 0], ALU.subtract).then_inc(s("wl_lo"), 1)
            pool.wait_ge(s("score"), 2 * NJ)
            for h in range(2):
                for e in range(2):
                    r = slice(64 * e, 64 * e + 64)
                    pool.memset(KL5[r, h, :, 1 - e, :].bitcast(U32), 0).then_inc(s("l_zero"), 1)
                    pool.wait_ge(s("l_zero"), 2 * h + e + 1)
            layernorm("l", 1)
            for h in range(H5):
                pool.wait_ge(s("vo_hi"), h + 1)
                pool.tensor_tensor(vo[:, h, 1], vo_stage[:, h % 4], vo[:, h, 0], ALU.subtract).then_inc(s("vo_lo"), 1)
            for b in range(B):
                layernorm("m", b)
            nh = col[:, COL["neghalf"]:COL["neghalf"] + 1].broadcast_to([P, 2])
            pool.wait_ge(s("m_qkv0"), 4)
            pool.wait_ge(s("m_qkv"), 2)
            queries_times_keys(pool, 1).then_inc(s("m_prod"), 1)
            for k, pair in enumerate((slice(0, NT, 2), slice(1, NT, 2), slice(0, 2), slice(2, 4))):
                pool.wait_ge(s("m_var"), k + 1)
                pool.tensor_tensor(rstd4[:, pair], mv4[:, pair, 1], nh, ALU.pow).then_inc(s("m_rstd"), 1)

        @block.vector
        def _(dve):
            steps = [0]

            def link(ins):
                steps[0] += 1
                ins.then_inc(s("dve_chain"), 1)
                dve.wait_ge(s("dve_chain"), steps[0])

            told = {}

            def publish(ins, name):
                told[name] = told.get(name, 0) + 1
                ins.then_inc(s(name), 1)
                dve.wait_ge(s(name), told[name])

            C = lambda name, n=P: col[0:n, COL[name]:COL[name] + 1]

            def layernorm(what, b, to=None):
                k = NORM[what, b]
                to = xn if to is None else to
                if what == "x":
                    dve.wait_ge(s("x_in%d" % b), 16)
                for t in range(2):
                    last = dve.bn_stats(bst[:, t, :], X[:, 2 * b + t, :])
                link(last)
                for t in range(2):
                    last = dve.bn_aggr(mv[:, t, :], bst[:, t, :])
                link(last)
                dve.tensor_scalar(mv[:, :, 1], mv[:, :, 1], EPS, None, ALU.add).then_inc(s("var"), 1)
                yield
                dve.wait_ge(s("rstd"), k + 1)
                if k:
                    dve.wait_ge(s("xn_turned"), k)
                for t in range(2):
                    last = dve.tensor_scalar(to[:, t, :], X[:, 2 * b + t, :], mv[:, t, 0:1], rstd[:, t:t + 1],
                                             ALU.subtract, ALU.mult)
                last.then_inc(s("xn"), 1)

            def turned(what, b):
                k = NORM[what, b]
                dve.wait_ge(s("xn_turned"), k + 1)
                dve.tensor_copy(xnT, bank(side_banks(what)[0], a=DC)).then_inc(s("xnT"), 1)

            def project(what, b):
                k = (what == "y") * B + b
                b0, b1, b2 = side_banks(what)
                yield from layernorm(what, b)
                yield
                turned(what, b)
                yield
                dve.wait_ge(s("px_q"), k + 1)
                if k >= 1:
                    dve.wait_ge(s("px_qt"), k)
                for e in range(DC):
                    last = dve.tensor_scalar(qT[:, e, :], ps[:, b1, e * SEQ:(e + 1) * SEQ], C("%s_bq%d" % (what, e)), None, ALU.add)
                last.then_inc(s("qT"), 1)
                yield
                dve.wait_ge(s("px_qt"), k + 1)
                r = slice(2 * b, 2 * b + 2)
                if k >= 2:
                    dve.wait_ge(s("exp"), (b + 1) * 2 * NCH)
                link(dve.tensor_copy(rq[:, r], ps[:, b0, 0:2]))
                dve.tensor_scalar(rqs[:, r], rq[:, r], SCALES[k // 2], SHIFT, ALU.mult, ALU.add)
                dve.wait_ge(s("qt_hi"), k + 1)
                dve.tensor_tensor(qtl[:, 1, :, b * SEQ:(b + 1) * SEQ], bank(b2, a=DC), qtl[:, 0, :, b * SEQ:(b + 1) * SEQ],
                                  ALU.subtract).then_inc(s("qt_lo"), 1)
                yield

            def linear_attention(b):
                dve.wait_ge(s("wa_in"), 48)
                yield from layernorm("a", b)
                yield
                turned("a", b)
                yield
                heads4 = lambda t: qk2[t].rearrange("p (g d) -> p g d", d=D2)
                for t in range(2):
                    n = 2 * b + t
                    dve.wait_ge(s("a_qkv"), n + 1)
                    dve.tensor_tensor(v2[:, t, :], ps[:, 3, t * D:(t + 1) * D], ba[:, 512:768], ALU.add)
                    link(dve.tensor_tensor(qk2[t], ps[:, 2 if t == 0 else 7, :], ba[:, 0:512], ALU.add))
                    yield
                    if n:
                        dve.wait_ge(s("a_sub"), n)
                    link(dve.tensor_reduce(s2[:, :], heads4(t), AX.X, ALU.max))
                    publish(dve.tensor_tensor(heads4(t), heads4(t), s2[:, :].unsqueeze(2).broadcast_to([P, P, D2]), ALU.subtract), "a_sub")
                yield
                for t in range(2):
                    dve.wait_ge(s("a_exp"), 2 * b + t + 1)
                    link(dve.tensor_reduce(s2[:, :], heads4(t), AX.X, ALU.add))
                    link(dve.reciprocal(s2[:, :], s2[:, :]))
                    publish(dve.tensor_tensor(heads4(t), heads4(t), s2[:, :].unsqueeze(2).broadcast_to([P, P, D2]), ALU.mult), "a_soft")
                    yield
                for _ in range(LA_WAIT - 3):
                    yield
                for t in range(2):
                    n = 2 * b + t
                    dve.wait_ge(s("a_cum"), n + 1)
                    q4 = qk2[t][:, 0:D].rearrange("p (h a) -> p h a", a=D2)
                    t4 = t2.rearrange("p (h a d) -> p h a d", a=D2, d=D2)
                    for half in range(2):
                        hs = slice(half * 32, half * 32 + 32)
                        cum = ps[:, 2 + half, :].rearrange("p (h a d) -> p h a d", a=D2, d=D2)
                        link(dve.tensor_tensor(t4, cum, q4[:, hs, :].unsqueeze(3).broadcast_to([P, 32, D2, D2]), ALU.mult))
                        link(dve.tensor_reduce(v2[:, t, half * P:(half + 1) * P].rearrange("p (h d) -> p h d", d=D2),
                                               t2.rearrange("p (h a d) -> p h d a", a=D2, d=D2), AX.X, ALU.add))
                        yield
                    link(dve.tensor_tensor(t2[:, 0:D], ps[:, 7, 0:D], qk2[t][:, 0:D], ALU.mult))
                    link(dve.tensor_reduce(s2[:, 0:H2], t2[:, 0:D].rearrange("p (h a) -> p h a", a=D2), AX.X, ALU.add))
                    link(dve.reciprocal(s2[:, 0:H2], s2[:, 0:H2]))
                    v3 = v2[:, t, :].rearrange("p (h d) -> p h d", d=D2)
                    dve.tensor_tensor(v3, v3, s2[:, 0:H2].unsqueeze(2).broadcast_to([P, H2, D2]), ALU.mult)\
                        .then_inc(s("a_o"), 1)
                    yield
                yield
                dve.wait_ge(s("a_out"), b + 1)
                xs = X[:, 2 * b:2 * b + 2, :]
                link(dve.tensor_tensor(xs, xs, bank(3, a=2), ALU.add))
                link(dve.tensor_tensor(xs, xs, ba[:, 768:1024].unsqueeze(1).broadcast_to([P, 2, D]), ALU.add))
                yield

            def feed_forward(b):
                dve.wait_ge(s("wf_in"), 112)
                if b == 0:
                    dve.tensor_copy(wf4, w41[:, 0:1].broadcast_to([64, P])).then_inc(s("wrep"), 1)
                    dve.tensor_copy(wg3, w41[:, 1:2].broadcast_to([64, P])).then_inc(s("wrep"), 1)
                yield from layernorm("f", b)
                yield
                turned("f", b)
                dve.wait_ge(s("xnT"), NORM["f", b] + 1)
                dve.tensor_reduce(gsum, xnT, AX.X, ALU.add).then_inc(s("f_sum"), 1)
                yield
                for i in range(CYCLES):
                    n = b * CYCLES + i
                    for _ in range(4):
                        yield
                    if i == 0:
                        dve.wait_ge(s("f_gs"), 3 * b + 3)
                        dve.tensor_scalar(cA, tg, cA7, 0.1, ALU.mult, ALU.add).then_inc(s("f_cA"), 1)
                        dve.wait_ge(s("f_cA"), b + 1)
                    dve.wait_ge(s("f_th"), n + 1)
                    link(dve.tensor_scalar(cpl, th, cB, cA, ALU.mult, ALU.add))
                    dve.scalar_tensor_tensor(tw[:, 0, :], xnT[:, 1, :], C("sgn0"), cpl, ALU.mult, ALU.mult)
                    link(dve.scalar_tensor_tensor(tw[:, 1, :], xnT[:, 0, :], C("sgn1"), cpl, ALU.mult, ALU.mult))
                    publish(dve.tensor_tensor(xnT, xnT, tw, ALU.add), "f_x")
                    yield
                dve.wait_ge(s("f_back"), b + 1)
                xs = X[:, 2 * b:2 * b + 2, :]
                link(dve.tensor_tensor(xs, xs, bank(2, a=2), ALU.add))
                yield

            def side(b):
                yield from linear_attention(b)
                yield from feed_forward(b)
                yield from project("y", b)

            def cut_lo(g):
                if g >= POOL_CUTS:
                    return
                dve.wait_ge(s("ctx_in%d" % (g % 2)), 16 * (g // 2 + 1))
                dve.wait_ge(s("ctx_hi"), g + 1)
                dve.tensor_tensor(CN[:, g * KT:(g + 1) * KT, 1, :], stage[:, g % 2], CN[:, g * KT:(g + 1) * KT, 0, :],
                                  ALU.subtract).then_inc(s("ctx_lo"), 1)

            def prep_out(g):
                dve.wait_ge(s("ctT_ps"), g + 1)
                dve.tensor_copy(CT[:, :, 1, g * CH:(g + 1) * CH].bitcast(U32),
                                ps[:, 3, :].bitcast(U32).rearrange("p (c k) -> p c k", c=DC)).then_inc(s("ctT_lo"), 1)

            def score_max(L, u, c):
                n = L * NJ + u * NCH + c
                dve.wait_ge(s("score_copied"), n + 1)
                dve.tensor_reduce(mx[:, u, c:c + 1], S[:, n % SRING, :], AX.X, ALU.max).then_inc(s("score_max"), 1)
                if c < NCH - 1:
                    return
                dve.wait_ge(s("score_max"), n + 1)
                link(dve.tensor_reduce(mrow[:, u:u + 1], mx[:, u, :], AX.X, ALU.max))
                link(dve.tensor_scalar(negb[:, u:u + 1], mrow[:, u:u + 1], rq[:, u:u + 1], -SCALES[L], ALU.add, ALU.mult))
                if L:
                    dve.wait_ge(s("exp"), (u + 1) * NCH)
                dve.tensor_tensor(ebias[:, u:u + 1], negb[:, u:u + 1], rqs[:, u:u + 1], ALU.add).then_inc(s("ebias"), 1)

            def pt_lo(L, u, c):
                j = L * NJ + u * NCH + c
                dve.wait_ge(s("pt_hi"), j + 1)
                dve.tensor_tensor(PL[j % PRING], ps[:, 4 + j % 2, :], PH[j % PRING], ALU.subtract).then_inc(s("pt_lo"), 1)

            def finish(L, u):
                dve.wait_ge(s("exp"), L * NJ + (u + 1) * NCH)
                link(dve.tensor_reduce(lsum[:, u:u + 1], ls[:, u, :], AX.X, ALU.add))
                link(dve.reciprocal(rl[:, u:u + 1], lsum[:, u:u + 1]))
                dve.wait_ge(s("av"), L * NJ + (u + 1) * NCH)
                if L == 0:
                    xs = X[:, u, :]
                    link(dve.scalar_tensor_tensor(xs, ps[:, acc_bank(u), 0:D], rl[:, u:u + 1], xs, ALU.mult, ALU.add))
                    publish(dve.scalar_tensor_tensor(xs, ps[:, acc_bank(u), D:2 * D], rl[:, u:u + 1], xs, ALU.mult, ALU.add), "acc_free")
                else:
                    if u:
                        dve.wait_ge(s("y_onT_ps"), u)
                    link(dve.tensor_scalar(on, ps[:, acc_bank(u), 0:D], rl[:, u:u + 1], None, ALU.mult))
                    dve.scalar_tensor_tensor(on, ps[:, acc_bank(u), D:2 * D], rl[:, u:u + 1], on, ALU.mult, ALU.add).then_inc(s("y_on"), 1)

            def finish_turn(u):
                dve.wait_ge(s("y_onT_ps"), u + 1)
                dve.tensor_copy(onT, ps[:, 6, 0:D].rearrange("p (c n) -> p c n", c=DC)).then_inc(s("y_onT"), 1)

            def finish_v(u):
                dve.wait_ge(s("y_v"), u + 1)
                dve.wait_ge(s("wyv_in"), 32)
                xs = X[:, u, :]
                link(dve.tensor_tensor(xs, xs, ps[:, 6, D:2 * D], ALU.add))
                publish(dve.tensor_tensor(xs, xs, byv, ALU.add), "acc_free")

            def attend(L, side_of):
                order = ORDER
                for i, (kind, u, c) in enumerate(order):
                    if L == 0 and i in PREP_AT:
                        g = PREP_AT.index(i) + 1
                        if g + 1 < NG:
                            cut_lo(g + 1)
                        prep_out(g)
                    if ahead(order, i, TURN):
                        pt_lo(L, *ahead(order, i, TURN))
                    side_steps(L, 2 * i, side_of)
                    if kind == "S":
                        score_max(L, u, c)
                    elif c == NCH - 1:
                        finish(L, u)
                    if L == 1 and finishes(order, i, 1) is not None:
                        finish_turn(finishes(order, i, 1))
                    if L == 1 and finishes(order, i, 2) is not None:
                        finish_v(finishes(order, i, 2))
                    if L == 1 and i + 1 == len(order):
                        finish_turn(u)
                        finish_v(u)
                    side_steps(L, 2 * i + 1, side_of)
                for _ in side_of:
                    pass

            def x_lo(b):
                dve.wait_ge(s("l_x_hi"), b + 1)
                dve.tensor_tensor(xl5[b][:, 1], xn, xl5[b][:, 0], ALU.subtract).then_inc(s("l_x_lo"), 1)

            def x_turned(b):
                dve.wait_ge(s("l_xT_hi"), b + 1)
                cols = slice(b * SEQ, (b + 1) * SEQ)
                dve.tensor_tensor(xT5[:, 1, :, cols], bank(side_banks("l", b)[0], a=DC), xT5[:, 0, :, cols], ALU.subtract)\
                    .then_inc(s("xnT"), 1)

            def enter_low_rank():
                yield from layernorm("l", 0)
                yield
                x_turned(0)
                yield
                x_lo(0)
                for _ in range(H5 // 2):
                    yield

            def low_rank_attention():
                dve.wait_ge(s("l_x_lo"), 1)
                for _ in layernorm("l", 1):
                    pass
                dve.wait_ge(s("l_zero"), 4)
                for b in range(B):
                    cols = slice(b * SEQ, (b + 1) * SEQ)
                    for j in range(H5 // 2):
                        n = b * (H5 // 2) + j
                        dve.wait_ge(s("l_hi"), n + 1)
                        dve.tensor_tensor(QL5[:, 1, j, cols], ps[:, n % 4, 0:SEQ], QL5[:, 0, j, cols], ALU.subtract)
                        for e in range(2):
                            r = slice(64 * e, 64 * e + 64)
                            o = dve.tensor_tensor(KL5[r, 1, j, e, cols], ps[r, n % 4, SEQ:2 * SEQ], KL5[r, 0, j, e, cols], ALU.subtract)
                        o.then_inc(s("l_lo"), 1)
                        if n == 2:
                            x_lo(1)
                            x_turned(1)

                def max5(i):
                    dve.wait_ge(s("l_score"), i + 1)
                    link(dve.tensor_reduce(nb5[:, i % 2, :], bank(i % 2, a=2), AX.X, ALU.max))
                    dve.tensor_scalar(nb5[:, i % 2, :], nb5[:, i % 2, :], -1.0 / 16, None, ALU.mult).then_inc(s("l_max"), 1)

                def lo5(i):
                    dve.wait_ge(s("l_pt_hi"), i + 1)
                    dve.tensor_tensor(ptl[:, i % 2, :], ps[:, 2 + i % 2, :], pth[:, i % 2, :], ALU.subtract)\
                        .then_inc(s("l_pt_lo"), 1)

                def norm5(i):
                    dve.wait_ge(s("l_exp"), 2 * i + 2)
                    link(dve.reciprocal(l5[:, i % 2, :], l5[:, i % 2, :]))
                    for t in range(2):
                        o = dve.tensor_scalar(P5[:, i % 2, t, :], P5[:, i % 2, t, :], l5[:, i % 2, t:t + 1], 1024.0, ALU.mult, ALU.mult)
                    o.then_inc(s("l_norm"), 1)

                def leave(b):
                    dve.wait_ge(s("l_vo"), (b + 1) * H5)
                    xs = X[:, 2 * b:2 * b + 2, :]
                    publish(dve.scalar_tensor_tensor(xs, bank(6 + b, a=2), 1.0 / (1024 * VO_SCALE), xs, ALU.mult, ALU.add), "x5")

                def enter_last():
                    leave(0)
                    yield
                    yield from layernorm("m", 0, x0[:, 0:2, :])
                    yield
                    dve.wait_ge(s("xn_turned"), NORM["m", 0] + 1)
                    dve.tensor_copy(x0T[:, :, 0:SEQ], bank(6, a=DC)).then_inc(s("m_xT"), 1)
                    yield
                    dve.wait_ge(s("w6_in"), 16 * 14)
                    for n in range(4):
                        t, a, z = n // 2, *((0, 512), (512, 768))[n % 2]
                        dve.wait_ge(s("m_qkv0_ps"), n + 1)
                        dve.tensor_tensor(qkv[:, t, a:z], ps[:, 6, 0:z - a], b6i[:, a:z], ALU.add).then_inc(s("m_qkv0"), 1)
                        yield

                early = enter_last()

                def oT_lo(i):
                    dve.wait_ge(s("l_ot_hi"), i + 1)
                    dve.tensor_tensor(oT5[:, i % 2, 1], bank(4 + i % 2, a=DC), oT5[:, i % 2, 0], ALU.subtract)\
                        .then_inc(s("l_ot_lo"), 1)

                for i in range(2 * H5 + 3):
                    if i < 2 * H5:
                        max5(i)
                    if 1 <= i <= 2 * H5:
                        norm5(i - 1)
                    if 2 <= i <= 2 * H5 + 1:
                        lo5(i - 2)
                    if i >= 3:
                        oT_lo(i - 3)
                    if i >= H5 + 4:
                        next(early, None)
                leave(1)

            def norm_stats(a, k, tiles):
                for t in tiles:
                    o = dve.bn_stats(bst4[:, t, :], a[:, t, :])
                link(o)
                for t in tiles:
                    o = dve.bn_aggr(mv4[:, t, :], bst4[:, t, :])
                link(o)
                pair = slice(tiles[0], tiles[1] + 1, tiles[1] - tiles[0])
                dve.tensor_scalar(mv4[:, pair, 1], mv4[:, pair, 1], EPS, None, ALU.add).then_inc(s("m_var"), 1)

            def norm_apply(a, k, tiles, g, to, beta):
                for t in tiles:
                    o = dve.scalar_tensor_tensor(a[:, t, :], a[:, t, :], mv4[:, t, 0:1], g, ALU.subtract, ALU.mult)
                link(o)
                dve.wait_ge(s("m_rstd"), k + 1)
                for t in tiles:
                    o = dve.scalar_tensor_tensor(to[:, t, :], a[:, t, :], rstd4[:, t:t + 1], beta(t), ALU.mult, ALU.add)
                return o

            def last_attention():
                dve.tensor_copy(ones16, ones[:, :])
                dve.tensor_copy(tris16, tris)
                dve.tensor_copy(id16, ident).then_inc(s("id16"), 1)
                dve.wait_ge(s("l_pv"), 2 * H5)
                for _ in layernorm("m", 1, x0[:, 2:4, :]):
                    pass
                dve.wait_ge(s("xn_turned"), NORM["m", 1] + 1)
                dve.tensor_copy(x0T[:, :, SEQ:2 * SEQ], bank(3, a=DC)).then_inc(s("m_xT"), 1)
                dve.wait_ge(s("m_qkv0"), 4)

                def qkv_out(j):
                    dve.wait_ge(s("m_qkv_ps"), j + 1)
                    publish(dve.tensor_tensor(qkv[:, 2 + j, :], ps[:, 4 * j:4 * j + 2, :].rearrange("p b n -> p (b n)")[:, 0:768],
                                              b6i, ALU.add), "m_qkv")

                def scores6(j):
                    link(dve.tensor_reduce(sc[:, j].rearrange("p l m h -> p (l m h)"), prods[j].rearrange("p (g d) -> p g d", d=HD6),
                                           AX.X, ALU.add))
                    both = smx[:, j].unsqueeze(2).broadcast_to([P, 2, 2, H6])
                    link(dve.tensor_tensor(smx[:, j], sc[:, j, :, 0, :], sc[:, j, :, 1, :], ALU.max))
                    publish(dve.tensor_tensor(sc[:, j], sc[:, j], both, ALU.subtract), "m_sub")

                def values6(j):
                    both = smx[:, j].unsqueeze(2).broadcast_to([P, 2, 2, H6])
                    dve.wait_ge(s("m_exp"), j + 1)
                    link(dve.tensor_tensor(smx[:, j], sc[:, j, :, 0, :], sc[:, j, :, 1, :], ALU.add))
                    link(dve.reciprocal(smx[:, j], smx[:, j]))
                    link(dve.tensor_tensor(sc[:, j], sc[:, j], both, ALU.mult))
                    part = prods[j][:, 0:512].rearrange("p (l d) -> p l d", l=2)
                    for m in range(2):
                        a = sc[:, j, :, m, :].unsqueeze(3).broadcast_to([P, 2, H6, HD6])
                        v = qkv[:, 2 * m + j, 512:768].rearrange("p (h d) -> p h d", h=H6).unsqueeze(1).broadcast_to([P, 2, H6, HD6])
                        to = o6[:, j:NT:2, :] if m == 0 else part
                        o = dve.tensor_tensor(to.rearrange("p l (h d) -> p l h d", h=H6), a, v, ALU.mult)
                    link(o)
                    publish(dve.tensor_tensor(o6[:, j:NT:2, :], o6[:, j:NT:2, :], part, ALU.add), "m_o")

                qkv_out(0)
                link(queries_times_keys(dve, 0))
                scores6(0)
                qkv_out(1)
                values6(0)
                dve.wait_ge(s("m_prod"), 1)
                scores6(1)
                for b in range(B):
                    dve.tensor_tensor(X[:, 2 * b:2 * b + 2, :], X[:, 2 * b:2 * b + 2, :],
                                      ln2b.unsqueeze(1).broadcast_to([P, 2, D]), ALU.add).then_inc(s("x_beta"), 1)
                values6(1)
                for j in range(2):
                    dve.wait_ge(s("m_out"), j + 1)
                    xs = x0[:, j:NT:2, :]
                    link(dve.tensor_tensor(xs, xs, bank(2 + j, a=2), ALU.add))
                    link(dve.tensor_tensor(xs, xs, b6o.unsqueeze(1).broadcast_to([P, 2, D]), ALU.add))
                    norm_stats(x0, j, (j, 2 + j))
                for j in range(2):
                    publish(norm_apply(x0, j, (j, 2 + j), ln1g, x0, lambda t: ln1b), "m_y1")

            def experts():
                for j in range(2):
                    dve.wait_ge(s("m_y1_hi"), j + 1)
                    dve.tensor_tensor(y1[:, 1, j:NT:2, :], x0[:, j:NT:2, :], y1[:, 0, j:NT:2, :], ALU.subtract).then_inc(s("m_y1_lo"), 1)
                dve.wait_ge(s("m_logit"), 1)
                by_e = lambda a: a.unsqueeze(2).broadcast_to([P, NT, E6])
                by_t = lambda a: a.unsqueeze(1).broadcast_to([P, NT, E6])
                link(dve.tensor_copy(lg, ps[:, 6, 0:NT * E6].rearrange("p (t e) -> p t e", t=NT)))
                link(dve.tensor_reduce(m8, lg, AX.X, ALU.max))
                dve.tensor_tensor(e8, lg, by_e(m8), ALU.subtract).then_inc(s("m_sub8"), 1)
                link(dve.tensor_tensor(t8, lg, by_e(m8), ALU.is_equal))
                link(dve.tensor_tensor(t8, t8, by_t(rev), ALU.mult))
                link(dve.tensor_reduce(mw, t8, AX.X, ALU.max))
                publish(dve.tensor_tensor(oh, t8, by_e(mw), ALU.is_equal), "m_oh")
                link(dve.tensor_tensor(u8, oh, by_t(e64), ALU.mult))
                link(dve.tensor_reduce(head, u8, AX.X, ALU.add))
                dve.wait_ge(s("m_cum"), 1)
                link(dve.tensor_tensor(t8, ps[:, 7, 0:NT * E6].rearrange("p (t e) -> p t e", t=NT), oh, ALU.mult))
                link(dve.tensor_reduce(slot, t8, AX.X, ALU.add))
                dve.tensor_scalar(over, slot, float(CAP), 4096.0, ALU.is_ge, ALU.mult)
                link(dve.tensor_tensor(head, slot, head, ALU.add))
                link(dve.tensor_tensor(slot, head, over, ALU.add))
                for t in range(NT):
                    dve.tensor_scalar(Sm[:, t, :], iota, slot[:, t:t + 1], None, ALU.is_equal).then_inc(s("m_S"), 1)
                dve.wait_ge(s("m_exp8"), 1)
                link(dve.tensor_reduce(gate, e8, AX.X, ALU.add))
                link(dve.reciprocal(gate, gate))
                dve.wait_ge(s("m_dis_ps"), 2)
                dve.wait_ge(s("m_dis"), 1)
                dve.tensor_copy(disT[:, 1, :], ps[:, 1, :]).then_inc(s("m_dis"), 1)
                for g in (1, 3):
                    dve.wait_ge(s("m_ST_ps"), g + 1)
                    dve.wait_ge(s("m_ST"), g)
                    dve.tensor_copy(ST[:, g, :].bitcast(U32), ps[:, 2 + g, 0:SEQ].bitcast(U32)).then_inc(s("m_ST"), 1)
                G = E6 // 2

                def h_out(g):
                    dve.wait_ge(s("m_h_ps"), g + 1)
                    dve.wait_ge(s("m_h"), 2 * g + 1)
                    if g >= 2:
                        dve.wait_ge(s("m_hT_ps"), g - 1)
                    dve.tensor_copy(hh[g % 2][:, 512:1024], ps[:, 1, :]).then_inc(s("m_h"), 1)

                def hT_out(g):
                    dve.wait_ge(s("m_hT_ps"), g + 1)
                    for f in range(2):
                        bias = b1c[:, 2 * g:2 * g + 2, 4 * f:4 * f + 4].rearrange("p e f -> p f e").unsqueeze(3)\
                            .broadcast_to([P, 4, 2, 64])
                        dve.tensor_tensor(hT[g % 2][:, 4 * f:4 * f + 4, :].rearrange("p f (e n) -> p f e n", e=2),
                                          ps[:, 2 + f, :].rearrange("p (f e n) -> p f e n", f=4, e=2), bias, ALU.add)\
                            .then_inc(s("m_hT"), 1)

                def y_out(g):
                    dve.wait_ge(s("m_y_ps"), g + 1)
                    publish(dve.tensor_tensor(ys, ps[:, 4, 0:D], b2r[:, g, :], ALU.add), "m_ys")
                    dve.wait_ge(s("m_y_hi"), g + 1)
                    dve.tensor_tensor(yy[:, g, 1], ys, yy[:, g, 0], ALU.subtract).then_inc(s("m_y"), 1)

                h_out(0)
                for g in range(G):
                    hT_out(g)
                    if g + 1 < G:
                        h_out(g + 1)
                    y_out(g)
                for b in range(B):
                    dve.wait_ge(s("m_comb"), b + 1)
                    tiles = (2 * b, 2 * b + 1)
                    for t in tiles:
                        o = dve.scalar_tensor_tensor(x0[:, t, :], ps[:, 6 + b, (t % 2) * D:(t % 2 + 1) * D], gate[:, t:t + 1],
                                                     x0[:, t, :], ALU.mult, ALU.add)
                    link(o)
                    norm_stats(x0, 2 + b, tiles)
                dve.wait_ge(s("x_beta"), B)
                for b in range(B):
                    norm_apply(x0, 2 + b, (2 * b, 2 * b + 1), ln2g, X, lambda t: X[:, t, :]).then_inc(s("x_final"), 1)

            dve.memset(ones[:, :], 1.0)
            dve.wait_ge(s("const_in"), 32)
            dve.tensor_copy(ident16[:, :], ident)
            dve.tensor_scalar(b4h, C("cn_b4"), 0.5, None, ALU.mult)
            dve.tensor_scalar(cA7, C("ar"), 0.7, None, ALU.mult)
            dve.tensor_scalar(cB, C("ar"), 0.3, None, ALU.mult)
            dve.tensor_scalar(b3h, C("gc_b3"), 0.5, None, ALU.mult).then_inc(s("halves"), 1)
            first = project("x", 0)
            for _ in range(3):
                next(first)
            cut_lo(0)
            next(first)
            prep_out(0)
            cut_lo(1)
            for _ in first:
                pass
            attend(0, chain(project("x", 1), side(0)))
            attend(1, chain(side(1), enter_low_rank()))
            low_rank_attention()
            last_attention()
            experts()


def chunked(w):
    return w.reshape(-1, P, w.shape[-1]).transpose(1, 0, 2)


def lay_out(x, ctx_1024, **w):
    cat = np.concatenate
    a = {}
    a["x"] = x.reshape(N, D)
    a["ctx"] = ctx_1024.reshape(B * KV, D)
    k = np.arange(P)
    a["consts"] = np.stack([k[:, None] == k, k[:, None] <= k, k[:, None] < k], 1).astype(np.float32)
    rep = lambda v: np.broadcast_to(v, (P,))
    pad = lambda v: np.concatenate([v, np.zeros(P - len(v), v.dtype)])
    sgn = np.where(k < P // 2, 1, -1).astype(np.float32)
    a["cols"] = np.stack([
        *w["L0_xattn_bq"].reshape(2, P), *w["L0_xattn_bk"].reshape(2, P), *w["L1_xattn_bq"].reshape(2, P),
        *w["L1_xattn_bk"].reshape(2, P), *w["L0_ffn_cn_b1"].reshape(2, P), w["L0_ffn_cn_b2"], pad(w["L0_ffn_cn_b3"]),
        rep(w["L0_ffn_cn_b4"]), w["L0_ffn_gc_b1"], pad(w["L0_ffn_gc_b2"]), rep(w["L0_ffn_gc_b3"]), rep(w["L0_attn_beta"]),
        rep(w["L0_ffn_adaptive_range"]), sgn, -sgn, np.full(P, -0.5, np.float32)], 1)
    a["w_x"] = np.stack([chunked(w["L0_xattn_Wq"].T), chunked(w["L0_xattn_Wk"])], 1)
    a["w_a"] = chunked(cat([w["L0_attn_Wq"].T, w["L0_attn_Wk"].T, w["L0_attn_Wv"].T], 1))
    a["w_ao"] = chunked(w["L0_attn_Wo"].T)
    a["b_a"] = cat([w["L0_attn_bq"], w["L0_attn_bk"], w["L0_attn_bv"], w["L0_attn_bo"]])
    a["w_f1"], a["w_f2"], a["w_f3"], a["w_f4"] = chunked(w["L0_ffn_cn_w1"]), chunked(w["L0_ffn_cn_w2"]), w["L0_ffn_cn_w3"], w["L0_ffn_cn_w4"]
    a["w_g1"], a["w_g2"], a["w_g3"] = chunked(w["L0_ffn_gc_w1"]), w["L0_ffn_gc_w2"], w["L0_ffn_gc_w3"]
    a["w_y"] = np.stack([chunked(w["L1_xattn_Wq"]), chunked(w["L1_xattn_Wk"].T)], 1)
    a["w_yv"], a["b_yv"] = chunked(w["L1_xattn_Wv"]), w["L1_xattn_bv"]
    qk = np.stack([w["L1_attn_Q"].reshape(H5 // 2, P, DC, P), w["L1_attn_K"].reshape(H5 // 2, P, DC, P)])
    a["w_l"] = qk.transpose(4, 1, 3, 0, 2).reshape(P, H5 // 2, DC, 2 * P)
    a["w_vo"] = w["L1_attn_VO"]
    a["w_in"], a["w_out"] = chunked(w["L1_ffn_in_proj_w"].T), chunked(w["L1_ffn_out_proj_w"].T)
    a["rows6"] = cat([w["L1_ffn_in_proj_b"], w["L1_ffn_out_proj_b"], w["L1_ffn_ln1_g"], w["L1_ffn_ln1_b"], w["L1_ffn_ln2_g"],
                      w["L1_ffn_ln2_b"]])
    a["w_gate"] = chunked(w["L1_ffn_wg"])
    a["w_e1"] = w["L1_ffn_w1"]
    a["b_e1"] = w["L1_ffn_b1"].reshape(E6, FC, P).transpose(2, 0, 1)
    a["w_e2"] = w["L1_ffn_w2"]
    a["b_e2"] = w["L1_ffn_b2"]
    a["consts6"] = np.broadcast_to(cat([np.arange(512), 8 - np.arange(8), CAP * np.arange(8)]).astype(np.float32), (P, 528))
    return {n: np.ascontiguousarray(v) for n, v in a.items()}


def kernel(**inputs):
    import concourse.bacc as bacc
    from concourse.bass_utils import run_bass_kernel_spmd as run

    arrays = lay_out(**{k: np.asarray(v) for k, v in inputs.items()})
    nc = bacc.Bacc("TRN2", target_bir_lowering=False, num_devices=1)
    args = {n: nc.dram_tensor("in_" + n, a.shape, mybir.dt.from_np(a.dtype), kind="ExternalInput").ap() for n, a in arrays.items()}
    out = nc.dram_tensor("out", (N, D), F32, kind="ExternalOutput").ap()
    build(nc, out=out, **args)
    r = run(nc, [{"in_" + n: a for n, a in arrays.items()}], core_ids=[0])
    return r.results[0]["out"].reshape(B, SEQ, D)
```
